# Optimizing a Trainium2 kernel written in Bass

```python
import numpy as np
import jax
import jax.numpy as jnp

def _softmax(x, axis=-1):
    return jax.nn.softmax(x, axis=axis)

def _gelu(x):
    return jax.nn.gelu(x, approximate=True)

def _silu(x):
    return jax.nn.silu(x)

def _sigmoid(x):
    return jax.nn.sigmoid(x)

def _layernorm(x, axis=-1, eps=1e-05):
    m = jnp.mean(x, axis=axis, keepdims=True)
    v = jnp.var(x, axis=axis, keepdims=True)
    return (x - m) / jnp.sqrt(v + eps)

def _scatter_add(tgt, idx, src, axis=0):
    return tgt.at[idx].add(src)

def _segment_sum(src, seg, n):
    return jax.ops.segment_sum(src, seg, n)
kernel_name = 'mk_adj_resnorm_d2_adj_r2_e395fe'

def setup_inputs(seed: int=0):
    np.random.seed(seed)
    _w = jnp.asarray

    def _rec_inputs():
        import jax
        import jax.numpy as jnp
        _gk = jax.random.key(seed)
        x = -0.000929 + 1 * jax.random.normal(jax.random.fold_in(_gk, 1), (4096, 128), jnp.float32)
        _w = (1.0 + jnp.arange(4096, dtype=jnp.float32)) ** (-0.5)
        _w = _w / _w.mean()
        _pij = jnp.clip(0.000488281 * _w[:, None] * _w[None, :], 0.0, 1.0)
        _a = jax.random.uniform(jax.random.fold_in(_gk, 2), (4096, 4096)) < _pij
        _a = jnp.logical_or(_a, jnp.swapaxes(_a, -1, -2))
        _a = jnp.logical_or(_a, jnp.eye(4096, dtype=bool))
        _af = _a.astype(jnp.float32)
        _af = _af * jax.random.uniform(jax.random.fold_in(_gk, 3), (4096, 4096), jnp.float32, 0.05, 0.0598829)
        adj = _af
        return (x, adj)
    x, adj = _rec_inputs()

    def _L0_gnn_setup():
        import jax, jax.numpy as jnp
        import numpy as np
        N, F_DIM, H_DIM = (4096, 128, 128)

        def _gwnn_layer(features, wavelets, wavelets_inv, W, filt):
            xw = features @ W
            spec = wavelets_inv @ xw
            spec = filt[:, None] * spec
            return wavelets @ spec
        key = jax.random.key(seed)
        ks = jax.random.split(key, 7)
        inp = {'input': jax.random.normal(ks[0], (N, F_DIM), dtype=jnp.float32), 'wavelets': jax.random.normal(ks[1], (N, N), dtype=jnp.float32) / np.sqrt(N), 'wavelets_inv': jax.random.normal(ks[2], (N, N), dtype=jnp.float32) / np.sqrt(N), 'W1': jax.random.uniform(ks[3], (F_DIM, H_DIM), dtype=jnp.float32, minval=-np.sqrt(6.0 / (F_DIM + H_DIM)), maxval=np.sqrt(6.0 / (F_DIM + H_DIM))), 'f1': jax.random.uniform(ks[4], (N,), dtype=jnp.float32, minval=0.9, maxval=1.1), 'W2': jax.random.uniform(ks[5], (H_DIM, H_DIM), dtype=jnp.float32, minval=-np.sqrt(6.0 / (H_DIM + H_DIM)), maxval=np.sqrt(6.0 / (H_DIM + H_DIM))), 'f2': jax.random.uniform(ks[6], (N,), dtype=jnp.float32, minval=0.9, maxval=1.1)}
        return inp
    _L0_gnn_all = _L0_gnn_setup()
    _L0_gnn_in = {k: v for k, v in _L0_gnn_all.items() if k in ('W1', 'f1', 'W2', 'f2')}
    del _L0_gnn_all

    def _L1_gnn_setup():
        import jax, jax.numpy as jnp
        import numpy as np
        N, D_IN, D_OUT = (4096, 128, 128)
        key = jax.random.key(seed)
        k1, k2, k3, k4, k5, k6 = jax.random.split(key, 6)
        bound = 1.0 / np.sqrt(D_IN)
        return {'h1': jax.random.normal(k1, (N, D_IN), dtype=jnp.float32), 'adj': jax.random.uniform(k2, (N, N), dtype=jnp.float32), 'negadj': jax.random.uniform(k3, (N, N), dtype=jnp.float32), 'W1': jax.random.uniform(k4, (D_OUT, D_IN), jnp.float32, -bound, bound), 'W2': jax.random.uniform(k5, (D_OUT, D_IN), jnp.float32, -bound, bound), 'Wf': jax.random.uniform(k6, (D_OUT, D_IN), jnp.float32, -bound, bound)}
    _L1_gnn_all = _L1_gnn_setup()
    _L1_gnn_in = {k: v for k, v in _L1_gnn_all.items() if k in ('W1', 'W2', 'Wf')}
    del _L1_gnn_all
    return {'x': x, 'adj': adj, 'L0_gnn_W1': _L0_gnn_in['W1'], 'L0_gnn_f1': _L0_gnn_in['f1'], 'L0_gnn_W2': _L0_gnn_in['W2'], 'L0_gnn_f2': _L0_gnn_in['f2'], 'L1_gnn_W1': _L1_gnn_in['W1'], 'L1_gnn_W2': _L1_gnn_in['W2'], 'L1_gnn_Wf': _L1_gnn_in['Wf']}

def reference(x, adj, L0_gnn_W1, L0_gnn_f1, L0_gnn_W2, L0_gnn_f2, L1_gnn_W1, L1_gnn_W2, L1_gnn_Wf):
    import jax
    import jax.numpy as jnp

    def _L0_gnn_ref(input, wavelets, wavelets_inv, W1, f1, W2, f2):
        import jax, jax.numpy as jnp
        import numpy as np
        N, F_DIM, H_DIM = (4096, 128, 128)

        def _gwnn_layer(features, wavelets, wavelets_inv, W, filt):
            xw = features @ W
            spec = wavelets_inv @ xw
            spec = filt[:, None] * spec
            return wavelets @ spec
        h1 = jax.nn.relu(_gwnn_layer(input, wavelets, wavelets_inv, W1, f1))
        out = _gwnn_layer(h1, wavelets, wavelets_inv, W2, f2)
        return out

    def _L1_gnn_ref(h1, adj, negadj, W1, W2, Wf):
        import jax, jax.numpy as jnp
        import numpy as np
        N, D_IN, D_OUT = (4096, 128, 128)
        h3 = h1 @ W1.T
        h4 = h1 @ W2.T
        hf = h1 @ Wf.T
        s = jax.nn.sigmoid(-(h3 @ h4.T))
        posx = s * adj
        negx = (1.0 - s) * negadj
        return hf + posx @ hf - negx @ hf
    x = _layernorm(x + _L0_gnn_ref(x, adj, adj, L0_gnn_W1, L0_gnn_f1, L0_gnn_W2, L0_gnn_f2), axis=-1)
    x = _layernorm(x + _L1_gnn_ref(x, adj, adj, L1_gnn_W1, L1_gnn_W2, L1_gnn_Wf), axis=-1)
    return x

_drawn_inputs = setup_inputs


def setup_inputs(seed=0):
    import zlib

    import numpy as np

    out = dict(_drawn_inputs(seed))
    spreads = {}
    factors = {'L0_gnn_W1': 8.0, 'L0_gnn_f1': 8.0, 'L0_gnn_W2': 8.0, 'L0_gnn_f2': 8.0}
    for name, (base, spread) in spreads.items():
        noise = np.random.default_rng([zlib.crc32(name.encode()), seed]).standard_normal(out[name].shape)
        drawn = base * np.exp(spread * noise) if base else spread * noise
        out[name] = jnp.asarray(drawn.astype(out[name].dtype))
    for name, factor in factors.items():
        out[name] = (out[name] * factor).astype(out[name].dtype)
    return out
```

```python
import numpy as np
import concourse.bass as bass
import concourse.mybir as mybir

F32 = mybir.dt.float32
F32R = mybir.dt.float32r
ALU = mybir.AluOpType
ACT = mybir.ActivationFunctionType

P = 128
N = 4096
D = 128
IB = 512
NI = N // IB
RC = IB // P
TC = 2
TW = TC * IB
NT = N // (TC * P)
KEPT = 2
NS = NT - KEPT
RING = 7
SPLITS = 4
TANHS = 4
POOL_TILES = (5, 11)
NPL = len(POOL_TILES)
NVL = NT - NPL
LAST = 4
EPS = 1e-5


def build(nc, adj, x_rows, x_cols, weights, filters, identity, out):
    base = nc.sbuf_base
    place = [(base + 31) // 32 * 32]

    def sb(name, free, dtype, at=None):
        if at is None:
            at = place[0]
            place[0] += -(-free * 4 // 32) * 32
        return nc.alloc_sbuf_tensor_at(name, [P, free], dtype, offset=at), at

    v = [[None, None], [None, None]]
    v[0][0], _ = sb("v_even_high", N, F32R)
    v[0][1], _ = sb("v_even_low", N, F32R)
    v[1][0], odd_at = sb("v_odd_high", N, F32R)
    v[1][1], odd_low_at = sb("v_odd_low", N, F32R)
    x_t, _ = sb("x_t", N, F32, odd_at)
    tanh_tiles, _ = sb("tanh_tiles", TANHS * TW, F32, odd_at)
    late_tiles, _ = sb("late_tiles", KEPT * TW, F32, odd_low_at)
    kept, kept_at = sb("kept", NI * KEPT * TW, F32)
    kept_r, _ = sb("kept_r", NI * KEPT * TW, F32R, kept_at)
    KB = KEPT * TW
    H4_HIGH, H4_LOW, H3, RESIDUAL = 0, IB, 2 * IB, 3 * IB
    ring, _ = sb("ring", RING * TW, F32)
    high, _ = sb("high", SPLITS * TW, F32R)
    low, _ = sb("low", SPLITS * TW, F32R)
    h3_high, _ = sb("h3_high", 2 * IB, F32R)
    h3_low, _ = sb("h3_low", 2 * IB, F32R)
    out_t, _ = sb("out_t", IB, F32)
    rows, _ = sb("rows", IB, F32)
    x1_t, _ = sb("x1_t", IB, F32)
    w, _ = sb("w", 5 * D, F32)
    filt, _ = sb("filt", 2 * NI * RC, F32)
    ident, _ = sb("ident", P, F32)
    stats, _ = sb("stats", RC * 6, F32)
    moments, _ = sb("moments", RC * 2, F32)
    variance, _ = sb("variance", RC, F32)
    rstd, _ = sb("rstd", RC, F32)
    power, _ = sb("power", RC, F32)
    assert place[0] <= nc.sbuf_usable_end, (place[0], nc.sbuf_usable_end)

    acc = nc.alloc_psum_tensor("acc", [P, 2 * IB], F32)
    score = nc.alloc_psum_tensor("score", [P, 2 * TW], F32)
    small = nc.alloc_psum_tensor("small", [P, IB], F32)
    small2 = nc.alloc_psum_tensor("small2", [P, IB], F32)

    sem = {}
    for name in (
        "weights_loaded", "late_loaded", "x_loaded", "stored",
        "tile_used", "acc_ready", "rows_ready", "x1t_ready", "h34_ready", "score_ready",
        "high_ready", "out_t_ready", "v_high_ready", "x1t_copied", "h3_copied", "h4_high_ready",
        "h3_high_ready", "tanh_ready",
        "low_ready", "rows_taken", "v_low_ready", "stats_ready", "stats_seen", "moments_ready", "variance_ready",
        "norm_ready", "h4_low_ready", "h3_low_ready", "signed_ready",
        "power_ready", "pool_low_ready", "rstd_ready", "partial_ready", "residual_ready",
    ):
        sem[name] = nc.alloc_semaphore(name)
    ring_loaded = [nc.alloc_semaphore(f"ring_loaded{s}") for s in range(RING)]
    xt_loaded = [nc.alloc_semaphore(f"xt_loaded{g}") for g in range(NI)]

    def tile_in(t, block):
        if t < NS:
            return ring[:, (t % RING) * TW:(t % RING + 1) * TW]
        return kept[:, bass.ds(block * KB + (t - NS) * TW, TW)]

    def tile_in_last(t):
        if t < NS:
            return ring[:, (t % RING) * TW:(t % RING + 1) * TW]
        return late_tiles[:, (t - NS) * TW:(t - NS + 1) * TW]

    def split_slot(buffer, t):
        return buffer[:, (t % SPLITS) * TW:(t % SPLITS + 1) * TW]

    def tanh_slot(t):
        return tanh_tiles[:, (t % TANHS) * TW:(t % TANHS + 1) * TW]

    def bank(block):
        return acc[:, bass.ds((block % 2) * IB, IB)]

    def group(buffer, g):
        return buffer[:, bass.ds(g * IB, IB)]

    def kept_part(buffer, block, part):
        return buffer[:, bass.ds(block * KB + part, IB)]

    def chunk(c):
        return slice(c * D, (c + 1) * D)

    def weight(k):
        return w[:, k * D:(k + 1) * D]

    W1, W2, W3, W4, WF = range(5)

    def wait_tile_loaded(eng, b, t):
        eng.wait_ge(ring_loaded[t % RING], (b * 2 + (t // RING + 1)) * 16)

    def wait_low(eng, b, t):
        if t < 0:
            b, t = b - 1, t + NT
        if t in POOL_TILES:
            eng.wait_ge(sem["pool_low_ready"], b * NPL + (POOL_TILES.index(t) + 1))
        else:
            eng.wait_ge(sem["low_ready"], b * NVL + (t + 1 - sum(k <= t for k in POOL_TILES)))

    class Steps:
        def __init__(self, evacuate, transpose, take, split, split_low, norm, transpose2, x1t,
                     project, project_out, project2, h4_low, hf, hf_low):
            self.evacuate, self.transpose, self.take = evacuate, transpose, take
            self.split, self.split_low, self.norm = split, split_low, norm
            self.transpose2, self.x1t, self.project = transpose2, x1t, project
            self.project_out, self.project2, self.h4_low = project_out, project2, h4_low
            self.hf, self.hf_low = hf, hf_low

    AHEAD = Steps(evacuate=3, transpose=1, take=5, split=6, split_low=7, norm=6, transpose2=4, x1t=8,
                  project=6, project_out=10, project2=8, h4_low=11, hf=12, hf_low=13)
    CLOSE = Steps(evacuate=0, transpose=1, take=2, split=3, split_low=4, norm=3, transpose2=4, x1t=5,
                  project=6, project_out=7, project2=8, h4_low=8, hf=9, hf_low=10)
    H3_SPLIT = 11

    block = nc.Block()
    block.__enter__()

    @block.sync
    def _(sp):
        def load_tile(row, t):
            nc.sync.dma_start(ring[:, (t % RING) * TW:(t % RING + 1) * TW],
                              adj[bass.ds((row * NT + t) * P, P), :]).then_inc(ring_loaded[t % RING], 16)

        def load_pair(buffer, offset, row):
            dst = buffer[:, bass.ds(offset, KB)].rearrange("p (t n) -> p t n", t=KEPT)
            src = adj[bass.ds((row * NT + NS) * P, KEPT * P), :].rearrange("(t p) n -> p t n", p=P)
            nc.sync.dma_start(dst, src).then_inc(sem["late_loaded"], 16)

        def load_x(I):
            nc.sync.dma_start(kept_part(kept, I, RESIDUAL),
                              x_rows[bass.ds(I * P, P), :]).then_inc(sem["x_loaded"], 16)

        def store_rows(J):
            sp.wait_ge(sem["norm_ready"], NI + J + 1)
            nc.sync.dma_start(out[bass.ds(J * P, P), :], rows[:, :]).then_inc(sem["stored"], 16)

        nc.sync.dma_start(w[:, :], weights[:, :]).then_inc(sem["weights_loaded"], 16)
        nc.sync.dma_start(filt[:, :], filters[:, :]).then_inc(sem["weights_loaded"], 16)
        nc.sync.dma_start(ident[:, :], identity[:, :]).then_inc(sem["weights_loaded"], 16)

        def load_x_t(g):
            nc.sync.dma_start(x_t[:, g * IB:(g + 1) * IB],
                              x_cols[:, g * IB:(g + 1) * IB]).then_inc(xt_loaded[g], 16)

        load_x_t(0)
        for t in range(NS):
            if t >= RING:
                wait_low(sp, 0, t - RING)
            load_tile(0, t)
            if t + 1 < NI:
                load_x_t(t + 1)
            if t == RING:
                load_pair(kept, 0, 0)
        with sp.Fori(1, NI) as I:
            for t in range(NS):
                wait_low(sp, I if t >= RING else I - 1, (t - RING) % NS)
                load_tile(I, t)
                if t == RING:
                    sp.wait_ge(sem["late_loaded"], I * 16)
                    load_pair(kept, I * KB, I)
        for q in (1, 2):
            with sp.Fori(0, NI) as I:
                for t in range(NS):
                    wait_low(sp, I + (q * NI if t >= RING else q * NI - 1), (t - RING) % NS)
                    load_tile(I, t)
        for t in range(NS):
            wait_low(sp, 3 * NI if t >= RING else 3 * NI - 1, (t - RING) % NS)
            load_tile(0, t)
        with sp.Fori(1, NI) as I:
            for t in range(NS):
                wait_low(sp, I + (3 * NI if t >= RING else 3 * NI - 1), (t - RING) % NS)
                load_tile(I, t)
                if t == RING:
                    wait_low(sp, I + (3 * NI - 1), NT - 1)
                    load_x(I - 1)
        for t in range(NS):
            if t >= RING:
                sp.wait_ge(sem["signed_ready"], t - RING + 1)
            else:
                wait_low(sp, LAST * NI - 1, t + RING)
            load_tile(0, t)
            if t == RING:
                wait_low(sp, LAST * NI - 1, NT - 1)
                load_x(NI - 1)
            if t == RING + 1:
                sp.wait_ge(sem["acc_ready"], LAST * NI)
                load_pair(late_tiles, 0, 0)
        with sp.Fori(1, NI) as I:
            for t in range(NS):
                sp.wait_ge(sem["signed_ready"],
                           I * NT + (t - RING + 1 if t >= RING else t - RING + 1 - KEPT))
                load_tile(I, t)
                if t == RING + 1:
                    sp.wait_ge(sem["signed_ready"], I * NT)
                    load_pair(late_tiles, 0, I)
                if t == NS - 2:
                    store_rows(I - 1)
        store_rows(NI - 1)
        sp.wait_ge(sem["stored"], NI * 16)

    @block.tensor
    def _(pe):
        def project_x(g):
            pe.wait_ge(xt_loaded[g], 16)
            if g:
                pe.wait_ge(sem["v_low_ready"], g)
            for c in range(RC):
                last = nc.tensor.matmul(small[:, chunk(c)], lhsT=x_t[:, g * IB + c * P:g * IB + (c + 1) * P],
                                        rhs=weight(W1), start=True, stop=True)
            last.then_inc(sem["rows_ready"], 1)

        def product(q, I, t):
            b = I + q * NI
            wait_low(pe, b, t)
            for c in range(TC):
                J = t * TC + c
                v_high, v_low = (v[q % 2][half][:, J * D:(J + 1) * D] for half in (0, 1))
                a_high, a_low = (split_slot(buf, t)[:, c * IB:(c + 1) * IB] for buf in (high, low))
                nc.tensor.matmul(bank(I), lhsT=v_high, rhs=a_high, start=J == 0, stop=False)
                nc.tensor.matmul(bank(I), lhsT=v_high, rhs=a_low, start=False, stop=False)
                last = nc.tensor.matmul(bank(I), lhsT=v_low, rhs=a_high, start=False,
                                        stop=J == NT * TC - 1)
            last.then_inc(sem["tile_used"], 1)

        def sum_done(I, q):
            pe.wait_ge(sem["tile_used"], (I + q * NI) * NT + NT)
            pe.sem_inc(sem["acc_ready"], 1)

        def wait_bank(q, I):
            if q or not isinstance(I, int) or I >= 2:
                pe.wait_ge(sem["out_t_ready"], I + (q * NI - 1))

        def transposed_rows(q, J):
            pe.wait_ge(sem["out_t_ready"], J + (q * NI + 1))
            if q < LAST:
                pe.wait_ge(sem["rows_taken"], J + NI * (q + 1))
            if q == 3:
                if not (isinstance(J, int) and J == 0):
                    pe.wait_ge(sem["v_low_ready"], J + NI * LAST)
            if q == LAST:
                pe.wait_ge(sem["rows_taken"], J + NI * (q + 1))
                pe.wait_ge(sem["v_low_ready"], NI * (LAST + 1))
            for c in range(RC):
                if q == 1:
                    last = nc.tensor.matmul(small[:, chunk(c)], lhsT=out_t[:, c * P:(c + 1) * P],
                                            rhs=weight(W2), start=True, stop=True)
                else:
                    last = nc.tensor.transpose(small[:, chunk(c)], out_t[:, c * P:(c + 1) * P], ident[:, :])
            last.then_inc(sem["rows_ready"], 1)

        def transposed_x1(J):
            pe.wait_ge(sem["norm_ready"], J + 1)
            pe.wait_ge(sem["h4_low_ready"], J)
            for c in range(RC):
                last = nc.tensor.transpose(small2[:, c * P:(c + 1) * P], rows[:, chunk(c)], ident[:, :])
            last.then_inc(sem["x1t_ready"], 1)

        def scores_operands(J):
            pe.wait_ge(sem["x1t_copied"], J + 1)
            nc.tensor.matmul(small[:, :], lhsT=weight(W3), rhs=x1_t[:, :], start=True, stop=True)
            nc.tensor.matmul(small2[:, :], lhsT=weight(W4), rhs=x1_t[:, :],
                             start=True, stop=True).then_inc(sem["h34_ready"], 1)

        def value_rows(J):
            pe.wait_ge(sem["h3_copied"], J + 1)
            for c in range(RC):
                last = nc.tensor.matmul(small[:, chunk(c)], lhsT=x1_t[:, c * P:(c + 1) * P],
                                        rhs=weight(WF), start=True, stop=True)
            last.then_inc(sem["rows_ready"], 1)

        def epilogue(q, J, t, at):
            if t == at.transpose:
                transposed_rows(q, J)
            if q == 3 and t == at.transpose2:
                transposed_x1(J)
            if q == 3 and t == at.project:
                scores_operands(J)
            if q == 3 and t == at.project2:
                value_rows(J)

        def scores(I, t):
            if not (isinstance(I, int) and I == 0 and t < 2):
                pe.wait_ge(sem["tanh_ready"], I * NT + (t - 1))
            for c in range(TC):
                J = t * TC + c
                g, r = J // RC, J % RC
                at = g * KB + r * P
                h4_high = kept_r[:, at + H4_HIGH:at + H4_HIGH + P]
                h4_low = kept_r[:, at + H4_LOW:at + H4_LOW + P]
                z = score[:, (t % 2) * TW + c * IB:(t % 2) * TW + (c + 1) * IB]
                b_high, b_low = (buf[:, bass.ds((I % 2) * IB, IB)] for buf in (h3_high, h3_low))
                nc.tensor.matmul(z, lhsT=h4_high, rhs=b_high, start=True, stop=False)
                nc.tensor.matmul(z, lhsT=h4_high, rhs=b_low, start=False, stop=False)
                last = nc.tensor.matmul(z, lhsT=h4_low, rhs=b_high, start=False, stop=True)
            last.then_inc(sem["score_ready"], 1)

        pe.wait_ge(sem["weights_loaded"], 3 * 16)
        project_x(0)
        for t in range(NT):
            if t % TC == 0:
                if t // TC + 1 < NI:
                    project_x(t // TC + 1)
                pe.wait_ge(sem["v_low_ready"], t // TC + 1)
            product(0, 0, t)
        sum_done(0, 0)
        for q in range(LAST):
            if q:
                wait_bank(q, 0)
                for t in range(NT):
                    if t % TC == 0:
                        pe.wait_ge(sem["v_low_ready"], q * NI + t // TC + 1)
                    product(q, 0, t)
                    epilogue(q - 1, NI - 1, t, AHEAD)
                sum_done(0, q)
            with pe.Fori(0, NI - 1) as J:
                if q:
                    wait_bank(q, J + 1)
                else:
                    pe.wait_ge(sem["out_t_ready"], J)
                for t in range(NT):
                    product(q, J + 1, t)
                    epilogue(q, J, t, AHEAD)
                sum_done(J + 1, q)

        pe.wait_ge(sem["h3_low_ready"], 1)
        scores(0, 0)
        scores(0, 1)
        wait_bank(LAST, 0)
        for t in range(NT - 2):
            if (t + 2) % TC == 0:
                pe.wait_ge(sem["h4_low_ready"], (t + 2) // TC + 1)
            scores(0, t + 2)
            if t % TC == 0:
                pe.wait_ge(sem["v_low_ready"], LAST * NI + t // TC + 1)
            product(LAST, 0, t)
            epilogue(3, NI - 1, t, CLOSE)
        with pe.Fori(0, NI - 1) as J:
            pe.wait_ge(sem["h3_low_ready"], J + 2)
            pe.wait_ge(sem["v_low_ready"], (LAST + 1) * NI)
            for t in range(2):
                scores(J + 1, t)
                product(LAST, J, NT - 2 + t)
            sum_done(J, LAST)
            wait_bank(LAST, J + 1)
            for t in range(NT - 2):
                scores(J + 1, t + 2)
                product(LAST, J + 1, t)
                epilogue(LAST, J, t, CLOSE)
        product(LAST, NI - 1, NT - 2)
        product(LAST, NI - 1, NT - 1)
        sum_done(NI - 1, LAST)
        transposed_rows(LAST, NI - 1)

    @block.scalar
    def _(act):
        def split_high(q, I, t):
            b = I + q * NI
            if q == LAST:
                act.wait_ge(sem["signed_ready"], I * NT + (t + 1))
                src = tanh_slot(t)
            elif t < NS:
                wait_tile_loaded(act, b, t)
                src = tile_in(t, I)
            else:
                if q == 0 and t == NS:
                    act.wait_ge(sem["late_loaded"], (I + 1) * 16)
                src = tile_in(t, I)
            if not (q == 0 and isinstance(I, int) and t < SPLITS):
                act.wait_ge(sem["tile_used"], b * NT + (t + 1 - SPLITS))
            nc.scalar.copy(split_slot(high, t), src).then_inc(sem["high_ready"], 1)

        def tanh_of(I, t):
            act.wait_ge(sem["score_ready"], I * NT + (t + 1))
            if not (isinstance(I, int) and I == 0 and t < TANHS):
                wait_low(act, I + LAST * NI, t - TANHS)
            nc.scalar.activation(tanh_slot(t), score[:, (t % 2) * TW:(t % 2 + 1) * TW], ACT.Tanh,
                                 scale=-0.5).then_inc(sem["tanh_ready"], 1)

        def evacuate(q, J):
            act.wait_ge(sem["acc_ready"], J + (q * NI + 1))
            if not (q == 0 and isinstance(J, int) and J == 0):
                act.wait_ge(sem["rows_ready"],
                            {3: J * 2 + (NI + q * NI), LAST: J + (NI + q * NI + NI)}.get(q, J + (NI + q * NI)))
            func = ACT.Relu if q == 1 else ACT.Copy
            nc.scalar.activation(out_t[:, :], bank(J), func).then_inc(sem["out_t_ready"], 1)

        def operand_high(q, J):
            if q == 1:
                act.wait_ge(sem["rows_ready"], J + (NI + q * NI + 1))
                src = small[:, :]
            else:
                act.wait_ge(sem["rows_taken"], J + (NI + q * NI + 1))
                src = rows[:, :]
            nc.scalar.copy(group(v[(q + 1) % 2][0], J), src).then_inc(sem["v_high_ready"], 1)

        def copy_x1t(J):
            act.wait_ge(sem["x1t_ready"], J + 1)
            nc.scalar.copy(x1_t[:, :], small2[:, :]).then_inc(sem["x1t_copied"], 1)

        def copy_h34(J):
            act.wait_ge(sem["h34_ready"], J + 1)
            nc.scalar.copy(kept_part(kept, J, H3), small[:, :]).then_inc(sem["h3_copied"], 1)
            nc.scalar.copy(kept_part(kept_r, J, H4_HIGH), small2[:, :]).then_inc(sem["h4_high_ready"], 1)

        def hf_high(J):
            act.wait_ge(sem["rows_ready"], (J + 1) * 2 + LAST * NI)
            nc.scalar.copy(group(v[0][0], J), small[:, :]).then_inc(sem["v_high_ready"], 1)

        def h3_split(I, parity):
            nc.scalar.copy(h3_high[:, bass.ds(parity * IB, IB)],
                           kept_part(kept, I, H3)).then_inc(sem["h3_high_ready"], 1)

        def epilogue(q, J, t, at):
            if t == at.evacuate:
                evacuate(q, J)
            if q < 3 and t == (at.take if q == 1 else at.split):
                operand_high(q, J)
            if q == 3 and t == at.x1t:
                copy_x1t(J)
            if q == 3 and t == at.project_out:
                copy_h34(J)
            if q == 3 and t == at.hf:
                hf_high(J)

        for t in range(NT):
            if t % TC == 0:
                g = t // TC
                act.wait_ge(sem["rows_ready"], g + 1)
                nc.scalar.copy(group(v[0][0], g), small[:, :]).then_inc(sem["v_high_ready"], 1)
            split_high(0, 0, t)
        for q in range(LAST):
            if q:
                for t in range(NT):
                    split_high(q, 0, t)
                    epilogue(q - 1, NI - 1, t, AHEAD)
            with act.Fori(0, NI - 1) as J:
                for t in range(NT):
                    split_high(q, J + 1, t)
                    epilogue(q, J, t, AHEAD)
        act.wait_ge(sem["h3_copied"], 1)
        h3_split(0, 0)
        act.wait_ge(sem["acc_ready"], LAST * NI)
        tanh_of(0, 0)
        for t in range(NT - 1):
            tanh_of(0, t + 1)
            split_high(LAST, 0, t)
            epilogue(3, NI - 1, t, CLOSE)
            if t == H3_SPLIT:
                act.wait_ge(sem["h3_copied"], NI)
                h3_split(1, 1)
        with act.Fori(0, NI - 1) as J:
            tanh_of(J + 1, 0)
            split_high(LAST, J, NT - 1)
            for t in range(NT - 1):
                tanh_of(J + 1, t + 1)
                split_high(LAST, J + 1, t)
                epilogue(LAST, J, t, CLOSE)
                if t == H3_SPLIT:
                    h3_split((J + 2) % NI, J % 2)
        split_high(LAST, NI - 1, NT - 1)
        evacuate(LAST, NI - 1)

    @block.vector
    def _(dve):
        def split_low(q, I, t):
            if t in POOL_TILES:
                return
            dve.wait_ge(sem["high_ready"], I * NT + (q * NI * NT + t + 1))
            src = tanh_slot(t) if q == LAST else tile_in(t, I)
            nc.vector.tensor_tensor(split_slot(low, t), src, split_slot(high, t),
                                    ALU.subtract).then_inc(sem["low_ready"], 1)

        def signed(I, t):
            if t < NS:
                wait_tile_loaded(dve, I + LAST * NI, t)
            elif t == NS:
                dve.wait_ge(sem["late_loaded"], (I + (NI + 1)) * 16)
            dve.wait_ge(sem["tanh_ready"], I * NT + (t + 1))
            nc.vector.tensor_tensor(tanh_slot(t), tanh_slot(t), tile_in_last(t),
                                    ALU.mult).then_inc(sem["signed_ready"], 1)

        def scale_rows(q, J):
            dve.wait_ge(sem["rows_ready"], J + (NI + q * NI + 1))
            if not (q == 0 and isinstance(J, int) and J == 0):
                dve.wait_ge(sem["v_high_ready"], J + NI * (q + 1))
            f = filt[:, bass.ds(J * RC + (q // 2) * NI * RC, RC)]
            nc.vector.tensor_tensor(rows[:, :].rearrange("p (c d) -> p c d", c=RC),
                                    small[:, :].rearrange("p (c d) -> p c d", c=RC),
                                    f.rearrange("p (c o) -> p c o", o=1).to_broadcast([P, RC, D]),
                                    ALU.mult).then_inc(sem["rows_taken"], 1)

        def operand_low(q, J):
            dve.wait_ge(sem["v_high_ready"], J + (NI * (q + 1) + 1))
            if q in (0, 2):
                dve.wait_ge(sem["rows_taken"], J + (NI + q * NI + 1))
            src = small if q in (1, 3) else rows
            last = nc.vector.tensor_tensor(group(v[(q + 1) % 2][1], J), src[:, :],
                                           group(v[(q + 1) % 2][0], J), ALU.subtract)
            last.then_inc(sem["v_low_ready"], 1)
            if q == 1:
                dve.wait_ge(sem["v_low_ready"], J + (NI * (q + 1) + 1))
                dve.sem_inc(sem["rows_taken"], 1)

        def add_and_moments(q, J):
            n = J + (NI if q == LAST else 0)
            if q == LAST:
                dve.wait_ge(sem["rows_ready"], J + (NI + q * NI + NI + 1))
                dve.wait_ge(sem["residual_ready"], NI)
                if not (isinstance(J, int) and J == 0):
                    dve.wait_ge(sem["stored"], J * 16)
            else:
                dve.wait_ge(sem["rows_ready"], J * 2 + (NI + q * NI + 1))
                dve.wait_ge(sem["x_loaded"], (J + 1) * 16)
                if not (isinstance(J, int) and J == 0):
                    dve.wait_ge(sem["residual_ready"], J)
            taken = J + (NI + q * NI + 1)
            nc.vector.tensor_tensor(rows[:, :], small[:, :], kept_part(kept, J, RESIDUAL),
                                    ALU.add).then_inc(sem["rows_taken"], 1)
            dve.wait_ge(sem["rows_taken"], taken)
            for c in range(RC):
                last = nc.vector.bn_stats(stats[:, c * 6:(c + 1) * 6], rows[:, chunk(c)])
            last.then_inc(sem["stats_ready"], 1)
            dve.wait_ge(sem["stats_ready"], n + 1)
            dve.sem_inc(sem["stats_seen"], 1)
            for c in range(RC):
                last = nc.vector.bn_aggr(moments[:, c * 2:(c + 1) * 2], stats[:, c * 6:(c + 1) * 6])
            last.then_inc(sem["moments_ready"], 1)
            dve.wait_ge(sem["moments_ready"], n + 1)
            nc.vector.tensor_scalar(variance[:, :].rearrange("p (c o) -> p c o", o=1),
                                    moments[:, :].rearrange("p (c o) -> p c o", o=2)[:, :, 1:2],
                                    EPS, None, ALU.add).then_inc(sem["variance_ready"], 1)

        def norm(q, J):
            n = J + (NI if q == LAST else 0)
            dve.wait_ge(sem["rstd_ready"], n + 1)
            for c in range(RC):
                last = nc.vector.tensor_scalar(rows[:, chunk(c)], rows[:, chunk(c)],
                                               moments[:, c * 2:c * 2 + 1], rstd[:, c:c + 1],
                                               ALU.subtract, ALU.mult)
            last.then_inc(sem["norm_ready"], 1)

        def h4_low(J):
            dve.wait_ge(sem["h4_high_ready"], J + 1)
            nc.vector.tensor_tensor(kept_part(kept_r, J, H4_LOW), small2[:, :],
                                    kept_part(kept_r, J, H4_HIGH),
                                    ALU.subtract).then_inc(sem["h4_low_ready"], 1)

        def h3_split(I, parity, count):
            dve.wait_ge(sem["h3_high_ready"], count)
            nc.vector.tensor_tensor(h3_low[:, bass.ds(parity * IB, IB)], kept_part(kept, I, H3),
                                    h3_high[:, bass.ds(parity * IB, IB)],
                                    ALU.subtract).then_inc(sem["h3_low_ready"], 1)

        def epilogue(q, J, t, at):
            if q in (0, 2) and t == at.take:
                scale_rows(q, J)
            if q in (0, 2) and t == at.split_low:
                operand_low(q, J)
            if q == 1 and t == at.split:
                operand_low(q, J)
            if q >= 3 and t == at.take:
                add_and_moments(q, J)
            if q >= 3 and t == at.norm:
                norm(q, J)
            if q == 3 and t == at.h4_low:
                h4_low(J)
            if q == 3 and t == at.hf_low:
                operand_low(q, J)

        for t in range(NT):
            if t % TC == 0:
                g = t // TC
                dve.wait_ge(sem["v_high_ready"], g + 1)
                nc.vector.tensor_tensor(group(v[0][1], g), small[:, :], group(v[0][0], g),
                                        ALU.subtract).then_inc(sem["v_low_ready"], 1)
            split_low(0, 0, t)
        dve.wait_ge(sem["v_low_ready"], NI)
        dve.sem_inc(sem["rows_taken"], NI)
        for q in range(LAST):
            if q:
                for t in range(NT):
                    split_low(q, 0, t)
                    epilogue(q - 1, NI - 1, t, AHEAD)
            with dve.Fori(0, NI - 1) as J:
                for t in range(NT):
                    split_low(q, J + 1, t)
                    epilogue(q, J, t, AHEAD)
        h3_split(0, 0, 1)
        signed(0, 0)
        for t in range(NT - 1):
            signed(0, t + 1)
            split_low(LAST, 0, t)
            epilogue(3, NI - 1, t, CLOSE)
            if t == H3_SPLIT:
                h3_split(1, 1, 2)
        with dve.Fori(0, NI - 1) as J:
            signed(J + 1, 0)
            split_low(LAST, J, NT - 1)
            for t in range(NT - 1):
                signed(J + 1, t + 1)
                split_low(LAST, J + 1, t)
                epilogue(LAST, J, t, CLOSE)
                if t == H3_SPLIT:
                    h3_split((J + 2) % NI, J % 2, J + 3)
        split_low(LAST, NI - 1, NT - 1)
        add_and_moments(LAST, NI - 1)
        norm(LAST, NI - 1)

    @block.gpsimd
    def _(pool):
        def split_low(q, I, t):
            pool.wait_ge(sem["high_ready"], I * NT + (q * NI * NT + t + 1))
            src = tanh_slot(t) if q == LAST else tile_in(t, I)
            nc.gpsimd.tensor_tensor(split_slot(low, t), src, split_slot(high, t),
                                    ALU.subtract).then_inc(sem["pool_low_ready"], 1)

        def inverse_deviation(n):
            pool.wait_ge(sem["variance_ready"], n)
            nc.gpsimd.tensor_tensor(rstd[:, :], variance[:, :], power[:, :],
                                    ALU.pow).then_inc(sem["rstd_ready"], 1)

        def residual(J):
            pool.wait_ge(sem["v_low_ready"], J + (LAST * NI + 1))
            place = kept_part(kept, J, RESIDUAL)
            nc.gpsimd.tensor_tensor(place, rows[:, :], group(v[0][0], J),
                                    ALU.add).then_inc(sem["partial_ready"], 1)
            pool.wait_ge(sem["partial_ready"], J + 1)
            nc.gpsimd.tensor_tensor(place, place, group(v[0][1], J),
                                    ALU.add).then_inc(sem["residual_ready"], 1)

        nc.gpsimd.memset(power[:, :], -0.5).then_inc(sem["power_ready"], 1)
        pool.wait_ge(sem["power_ready"], 1)
        for q in range(3):
            with pool.Fori(0, NI) as I:
                for t in POOL_TILES:
                    split_low(q, I, t)
        for t in POOL_TILES:
            split_low(3, 0, t)
        with pool.Fori(0, NI - 1) as J:
            split_low(3, J + 1, POOL_TILES[0])
            inverse_deviation(J + 1)
            split_low(3, J + 1, POOL_TILES[1])
            residual(J)
        inverse_deviation(NI)
        for t in POOL_TILES:
            split_low(LAST, 0, t)
        residual(NI - 1)
        with pool.Fori(0, NI - 1) as J:
            inverse_deviation(J + (NI + 1))
            for t in POOL_TILES:
                split_low(LAST, J + 1, t)
        inverse_deviation(2 * NI)

    block.__exit__(None, None, None)


def kernel(x, adj, L0_gnn_W1, L0_gnn_f1, L0_gnn_W2, L0_gnn_f2, L1_gnn_W1, L1_gnn_W2, L1_gnn_Wf):
    import concourse.bacc as bacc
    from concourse.bass_utils import run_bass_kernel_spmd

    x, adj = np.asarray(x), np.asarray(adj)
    tiles = adj.reshape(NI, IB, NT, TC, P).transpose(0, 2, 4, 3, 1).reshape(NI * NT * P, TW)
    arrays = {
        "adj": tiles,
        "x_rows": x.reshape(NI, RC, P, D).transpose(0, 2, 1, 3).reshape(NI * P, IB),
        "x_cols": x.T,
        "weights": np.concatenate([np.asarray(L0_gnn_W1), np.asarray(L0_gnn_W2), np.asarray(L1_gnn_W1).T,
                                   np.asarray(L1_gnn_W2).T, np.asarray(L1_gnn_Wf).T], axis=1),
        "filters": np.concatenate([np.asarray(f).reshape(N // P, P).T for f in (L0_gnn_f1, L0_gnn_f2)], axis=1),
        "identity": np.eye(P, dtype=np.float32),
    }
    arrays = {k: np.ascontiguousarray(a) for k, a in arrays.items()}
    nc = bacc.Bacc("TRN2", target_bir_lowering=False, num_devices=1)
    handles = {k: nc.dram_tensor(k, a.shape, F32, kind="ExternalInput").ap() for k, a in arrays.items()}
    out = nc.dram_tensor("out", (NI * P, IB), F32, kind="ExternalOutput").ap()
    build(nc, handles["adj"], handles["x_rows"], handles["x_cols"], handles["weights"],
          handles["filters"], handles["identity"], out)
    result = run_bass_kernel_spmd(nc, [arrays], core_ids=[0])
    got = result.results[0]["out"]
    return got.reshape(NI, P, RC, D).transpose(0, 2, 1, 3).reshape(N, D)
```

```python
import numpy as np
import concourse.bass as bass
import concourse.mybir as mybir

F32 = mybir.dt.float32
F32R = mybir.dt.float32r
ALU = mybir.AluOpType
ACT = mybir.ActivationFunctionType

P = 128
N = 4096
D = 128
IB = 512
NI = N // IB
RC = IB // P
TC = 2
TW = TC * IB
NT = N // (TC * P)
KEPT = 2
NS = NT - KEPT
LEAD = 3
RING = 7
SPLITS = 4
TANHS = 4
POOL_PASS = 3
POOL_TILES = (5, 11)
LAST = 4
EPS = 1e-5


def build(nc, adj, x_rows, x_cols, weights, filters, identity, out):
    base = nc.sbuf_base
    place = [(base + 31) // 32 * 32]

    def sb(name, free, dtype, at=None):
        if at is None:
            at = place[0]
            place[0] += -(-free * 4 // 32) * 32
        return nc.alloc_sbuf_tensor_at(name, [P, free], dtype, offset=at), at

    v = [[None, None], [None, None]]
    v[0][0], _ = sb("v_even_high", N, F32R)
    v[0][1], _ = sb("v_even_low", N, F32R)
    v[1][0], odd_at = sb("v_odd_high", N, F32R)
    v[1][1], odd_low_at = sb("v_odd_low", N, F32R)
    x_t, _ = sb("x_t", N, F32, odd_at)
    tanh_tiles, _ = sb("tanh_tiles", TANHS * TW, F32, odd_at)
    late_tiles, _ = sb("late_tiles", KEPT * TW, F32, odd_low_at)
    kept, kept_at = sb("kept", NI * KEPT * TW, F32)
    kept_r, _ = sb("kept_r", NI * KEPT * TW, F32R, kept_at)
    KB = KEPT * TW
    H4_HIGH, H4_LOW, H3, RESIDUAL = 0, IB, 2 * IB, 3 * IB
    ring, _ = sb("ring", RING * TW, F32)
    high, _ = sb("high", SPLITS * TW, F32R)
    low, _ = sb("low", SPLITS * TW, F32R)
    h3_high, _ = sb("h3_high", 2 * IB, F32R)
    h3_low, _ = sb("h3_low", 2 * IB, F32R)
    out_t, _ = sb("out_t", IB, F32)
    rows, _ = sb("rows", IB, F32)
    x1_t, _ = sb("x1_t", IB, F32)
    w, _ = sb("w", 5 * D, F32)
    filt, _ = sb("filt", 2 * NI * RC, F32)
    ident, _ = sb("ident", P, F32)
    stats, _ = sb("stats", RC * 6, F32)
    moments, _ = sb("moments", RC * 2, F32)
    variance, _ = sb("variance", RC, F32)
    rstd, _ = sb("rstd", RC, F32)
    power, _ = sb("power", RC, F32)
    minus, _ = sb("minus", RC, F32)
    shift, _ = sb("shift", RC, F32)
    assert place[0] <= nc.sbuf_usable_end, (place[0], nc.sbuf_usable_end)

    acc = nc.alloc_psum_tensor("acc", [P, 2 * IB], F32)
    score = nc.alloc_psum_tensor("score", [P, 2 * TW], F32)
    small = nc.alloc_psum_tensor("small", [P, IB], F32)
    small2 = nc.alloc_psum_tensor("small2", [P, IB], F32)

    sem = {}
    for name in (
        "weights_loaded", "late_loaded", "x_loaded", "stored",
        "tile_used", "rows_ready", "x1t_ready", "h34_ready", "score_ready",
        "high_ready", "out_t_ready", "v_high_ready", "x1t_copied", "h3_copied", "h4_high_ready",
        "h3_high_ready", "tanh_ready", "norm_ready",
        "low_ready", "rows_taken", "v_low_ready", "stats_ready", "stats_seen", "moments_ready", "variance_ready",
        "h4_low_ready", "signed_ready", "last_norm_ready",
        "power_ready", "pool_low_ready", "rstd_ready", "partial_ready", "residual_ready", "h3_low_ready", "shift_ready", "minus_ready",
    ):
        sem[name] = nc.alloc_semaphore(name)
    ring_loaded = [nc.alloc_semaphore(f"ring_loaded{s}") for s in range(RING)]
    xt_loaded = [nc.alloc_semaphore(f"xt_loaded{g}") for g in range(NI)]

    def tile_in(t, block):
        if t < NS:
            return ring[:, (t % RING) * TW:(t % RING + 1) * TW]
        return kept[:, bass.ds(block * KB + (t - NS) * TW, TW)]

    def tile_in_last(t):
        if t < NS:
            return ring[:, (t % RING) * TW:(t % RING + 1) * TW]
        return late_tiles[:, (t - NS) * TW:(t - NS + 1) * TW]

    def split_slot(buffer, t):
        return buffer[:, (t % SPLITS) * TW:(t % SPLITS + 1) * TW]

    def tanh_slot(t):
        return tanh_tiles[:, (t % TANHS) * TW:(t % TANHS + 1) * TW]

    def bank(block):
        return acc[:, bass.ds((block % 2) * IB, IB)]

    def group(buffer, g):
        return buffer[:, bass.ds(g * IB, IB)]

    def kept_part(buffer, block, part):
        return buffer[:, bass.ds(block * KB + part, IB)]

    def chunk(c):
        return slice(c * D, (c + 1) * D)

    def weight(k):
        return w[:, k * D:(k + 1) * D]

    W1, W2, W3, W4, WF = range(5)

    def wait_tile_loaded(eng, b, t):
        eng.wait_ge(ring_loaded[t % RING], (b * 2 + (t // RING + 1)) * 16)

    def pool_tiles(q):
        return POOL_TILES if q == POOL_PASS else ()

    def wait_low(eng, q, I, t):
        if t < 0:
            I, t = I - 1, t + NT
            if isinstance(I, int) and I < 0:
                q, I = q - 1, NI - 1
        helped = pool_tiles(q)
        if t in helped:
            eng.wait_ge(sem["pool_low_ready"], I * len(helped) + (helped.index(t) + 1))
        else:
            before = NI * (NT * q - (len(POOL_TILES) if q > POOL_PASS else 0))
            eng.wait_ge(sem["low_ready"],
                        I * (NT - len(helped)) + (before + t + 1 - sum(k <= t for k in helped)))

    AHEAD = dict(evacuate=3, transpose=1, take=5, split=6, split_low=7, stats=6, moments=7, norm=9,
                 transpose2=8, x1t=10, project=10, project_out=12, project2=12, h4_low=13, hf=15,
                 hf_low=15)
    CLOSE = dict(evacuate=1, transpose=2, take=4, stats=5, moments=6, norm=9,
                 transpose2=9, x1t=10, project=10, project_out=11, project2=11, h4_low=11, hf=12,
                 hf_low=12)
    H3_SPLIT = 10

    block = nc.Block()
    block.__enter__()

    @block.sync
    def _(sp):
        def load_tile(row, t):
            nc.sync.dma_start(ring[:, (t % RING) * TW:(t % RING + 1) * TW],
                              adj[bass.ds((row * NT + t) * P, P), :]).then_inc(ring_loaded[t % RING], 16)

        def wait_slot(q, I, t):
            wait_low(sp, q, I, t - RING if t >= RING else t - RING - KEPT)

        def load_pair(buffer, offset, row):
            dst = buffer[:, bass.ds(offset, KB)].rearrange("p (t n) -> p t n", t=KEPT)
            src = adj[bass.ds((row * NT + NS) * P, KEPT * P), :].rearrange("(t p) n -> p t n", p=P)
            nc.sync.dma_start(dst, src).then_inc(sem["late_loaded"], 16)

        def load_x(I):
            nc.sync.dma_start(kept_part(kept, I, RESIDUAL),
                              x_rows[bass.ds(I * P, P), :]).then_inc(sem["x_loaded"], 16)

        def store_rows(J):
            sp.wait_ge(sem["norm_ready"], NI + J + 1)
            nc.sync.dma_start(out[bass.ds(J * P, P), :], rows[:, :]).then_inc(sem["stored"], 16)

        sp.sem_inc(sem["stored"], 16)
        nc.sync.dma_start(w[:, :], weights[:, :]).then_inc(sem["weights_loaded"], 16)
        nc.sync.dma_start(filt[:, :], filters[:, :]).then_inc(sem["weights_loaded"], 16)
        nc.sync.dma_start(ident[:, :], identity[:, :]).then_inc(sem["weights_loaded"], 16)

        def load_x_t(g):
            nc.sync.dma_start(x_t[:, g * IB:(g + 1) * IB],
                              x_cols[:, g * IB:(g + 1) * IB]).then_inc(xt_loaded[g], 16)

        load_x_t(0)
        for t in range(NS):
            if t >= RING:
                wait_low(sp, 0, 0, t - RING)
            load_tile(0, t)
            if t + 1 < NI:
                load_x_t(t + 1)
            if t == RING:
                load_pair(kept, 0, 0)
        with sp.Fori(1, NI) as I:
            for t in range(NS):
                wait_slot(0, I, t)
                load_tile(I, t)
                if t == RING:
                    sp.wait_ge(sem["late_loaded"], I * 16)
                    load_pair(kept, I * KB, I)
        for q in (1, 2):
            for t in range(NS):
                wait_slot(q, 0, t)
                load_tile(0, t)
            with sp.Fori(1, NI) as I:
                for t in range(NS):
                    wait_slot(q, I, t)
                    load_tile(I, t)
        for t in range(NS):
            wait_slot(3, 0, t)
            load_tile(0, t)
        with sp.Fori(1, NI) as I:
            for t in range(NS):
                wait_slot(3, I, t)
                load_tile(I, t)
                if t == RING:
                    wait_low(sp, 3, I, -1)
                    load_x(I - 1)
        for t in range(NS):
            if t >= RING:
                sp.wait_ge(sem["signed_ready"], t - RING + 1)
            else:
                wait_slot(LAST, 0, t)
            load_tile(0, t)
            if t == RING:
                wait_low(sp, LAST, 0, -1)
                load_x(NI - 1)
            if t == RING + 1:
                sp.wait_ge(sem["tile_used"], LAST * NI * NT)
                load_pair(late_tiles, 0, 0)
        with sp.Fori(1, NI) as I:
            for t in range(NS):
                sp.wait_ge(sem["signed_ready"],
                           I * NT + (t - RING + 1 if t >= RING else t - RING + 1 - KEPT))
                load_tile(I, t)
                if t == RING + 1:
                    sp.wait_ge(sem["signed_ready"], I * NT)
                    load_pair(late_tiles, 0, I)
                if t == NS - 2:
                    store_rows(I - 1)
        sp.wait_ge(sem["last_norm_ready"], 1)
        nc.sync.dma_start(out[(NI - 1) * P:NI * P, :], rows[:, :]).then_inc(sem["stored"], 16)
        sp.wait_ge(sem["stored"], (NI + 1) * 16)

    @block.tensor
    def _(pe):
        def project_x(g):
            pe.wait_ge(xt_loaded[g], 16)
            if g:
                pe.wait_ge(sem["v_low_ready"], g)
            for c in range(RC):
                last = nc.tensor.matmul(small[:, chunk(c)], lhsT=x_t[:, g * IB + c * P:g * IB + (c + 1) * P],
                                        rhs=weight(W1), start=True, stop=True)
            last.then_inc(sem["rows_ready"], 1)

        def product(q, I, t):
            wait_low(pe, q, I, t)
            for c in range(TC):
                J = t * TC + c
                v_high, v_low = (v[q % 2][half][:, J * D:(J + 1) * D] for half in (0, 1))
                a_high, a_low = (split_slot(buf, t)[:, c * IB:(c + 1) * IB] for buf in (high, low))
                nc.tensor.matmul(bank(I), lhsT=v_high, rhs=a_high, start=J == 0, stop=False)
                nc.tensor.matmul(bank(I), lhsT=v_high, rhs=a_low, start=False, stop=False)
                last = nc.tensor.matmul(bank(I), lhsT=v_low, rhs=a_high, start=False,
                                        stop=J == NT * TC - 1)
            last.then_inc(sem["tile_used"], 1)

        def transposed_rows(q, J):
            pe.wait_ge(sem["out_t_ready"], J + (q * NI + 1))
            if q < LAST:
                pe.wait_ge(sem["rows_taken"], J + NI * (q + 1))
            if q == 3:
                if not (isinstance(J, int) and J == 0):
                    pe.wait_ge(sem["v_low_ready"], J + NI * LAST)
            if q == LAST:
                pe.wait_ge(sem["rows_taken"], J + NI * (q + 1))
                pe.wait_ge(sem["v_low_ready"], NI * (LAST + 1))
            for c in range(RC):
                if q == 1:
                    last = nc.tensor.matmul(small[:, chunk(c)], lhsT=out_t[:, c * P:(c + 1) * P],
                                            rhs=weight(W2), start=True, stop=True)
                else:
                    last = nc.tensor.transpose(small[:, chunk(c)], out_t[:, c * P:(c + 1) * P], ident[:, :])
            last.then_inc(sem["rows_ready"], 1)

        def transposed_x1(J):
            pe.wait_ge(sem["norm_ready"], J + 1)
            for c in range(RC):
                last = nc.tensor.transpose(small2[:, c * P:(c + 1) * P], rows[:, chunk(c)], ident[:, :])
            last.then_inc(sem["x1t_ready"], 1)

        def scores_operands(J):
            pe.wait_ge(sem["x1t_copied"], J + 1)
            nc.tensor.matmul(small[:, :], lhsT=weight(W3), rhs=x1_t[:, :], start=True, stop=True)
            nc.tensor.matmul(small2[:, :], lhsT=weight(W4), rhs=x1_t[:, :],
                             start=True, stop=True).then_inc(sem["h34_ready"], 1)

        def value_rows(J):
            pe.wait_ge(sem["h3_copied"], J + 1)
            for c in range(RC):
                last = nc.tensor.matmul(small[:, chunk(c)], lhsT=x1_t[:, c * P:(c + 1) * P],
                                        rhs=weight(WF), start=True, stop=True)
            last.then_inc(sem["rows_ready"], 1)

        def epilogue(q, J, t, at):
            if t == at["transpose"]:
                transposed_rows(q, J)
            if q == 3 and t == at["transpose2"]:
                transposed_x1(J)
            if q == 3 and t == at["project"]:
                scores_operands(J)
            if q == 3 and t == at["project2"]:
                value_rows(J)

        def scores(I, t):
            if not (isinstance(I, int) and I == 0 and t < 2):
                pe.wait_ge(sem["tanh_ready"], I * NT + (t - 1))
            for c in range(TC):
                J = t * TC + c
                g, r = J // RC, J % RC
                at = g * KB + r * P
                h4_high = kept_r[:, at + H4_HIGH:at + H4_HIGH + P]
                h4_low = kept_r[:, at + H4_LOW:at + H4_LOW + P]
                z = score[:, (t % 2) * TW + c * IB:(t % 2) * TW + (c + 1) * IB]
                b_high, b_low = (buf[:, bass.ds((I % 2) * IB, IB)] for buf in (h3_high, h3_low))
                nc.tensor.matmul(z, lhsT=h4_high, rhs=b_high, start=True, stop=False)
                nc.tensor.matmul(z, lhsT=h4_high, rhs=b_low, start=False, stop=False)
                last = nc.tensor.matmul(z, lhsT=h4_low, rhs=b_high, start=False, stop=True)
            last.then_inc(sem["score_ready"], 1)

        pe.wait_ge(sem["weights_loaded"], 3 * 16)
        project_x(0)
        for t in range(NT):
            if t % TC == 0:
                if t // TC + 1 < NI:
                    project_x(t // TC + 1)
                pe.wait_ge(sem["v_low_ready"], t // TC + 1)
            product(0, 0, t)
        for q in range(LAST):
            if q:
                for t in range(NT):
                    if t % TC == 0:
                        pe.wait_ge(sem["v_low_ready"], q * NI + t // TC + 1)
                    product(q, 0, t)
                    epilogue(q - 1, NI - 1, t, AHEAD)
            with pe.Fori(0, NI - 1) as J:
                for t in range(NT):
                    product(q, J + 1, t)
                    epilogue(q, J, t, AHEAD)

        pe.wait_ge(sem["h3_low_ready"], 1)
        for t in range(LEAD):
            scores(0, t)
        for t in range(NT - LEAD):
            if (t + LEAD) % TC == 0:
                pe.wait_ge(sem["h4_low_ready"], (t + LEAD) // TC + 1)
            scores(0, t + LEAD)
            if t % TC == 0:
                pe.wait_ge(sem["v_low_ready"], LAST * NI + t // TC + 1)
            product(LAST, 0, t)
            epilogue(3, NI - 1, t, CLOSE)
        with pe.Fori(0, NI - 1) as J:
            pe.wait_ge(sem["h3_low_ready"], J + 2)
            pe.wait_ge(sem["v_low_ready"], (LAST + 1) * NI)
            for t in range(LEAD):
                scores(J + 1, t)
                product(LAST, J, NT - LEAD + t)
            for t in range(NT - LEAD):
                scores(J + 1, t + LEAD)
                product(LAST, J + 1, t)
                epilogue(LAST, J, t, CLOSE)
        for t in range(NT - LEAD, NT):
            product(LAST, NI - 1, t)
        transposed_rows(LAST, NI - 1)

    @block.scalar
    def _(act):
        def split_high(q, I, t):
            b = I + q * NI
            if q == LAST:
                act.wait_ge(sem["signed_ready"], I * NT + (t + 1))
                src = tanh_slot(t)
            elif t < NS:
                wait_tile_loaded(act, b, t)
                src = tile_in(t, I)
            else:
                if q == 0 and t == NS:
                    act.wait_ge(sem["late_loaded"], (I + 1) * 16)
                src = tile_in(t, I)
            if not (q == 0 and isinstance(I, int) and t < SPLITS):
                act.wait_ge(sem["tile_used"], b * NT + (t + 1 - SPLITS))
            nc.scalar.copy(split_slot(high, t), src).then_inc(sem["high_ready"], 1)

        def tanh_of(I, t):
            act.wait_ge(sem["score_ready"], I * NT + (t + 1))
            if not (isinstance(I, int) and I == 0 and t < TANHS):
                wait_low(act, LAST, I, t - TANHS)
            nc.scalar.activation(tanh_slot(t), score[:, (t % 2) * TW:(t % 2 + 1) * TW], ACT.Tanh,
                                 scale=-0.5).then_inc(sem["tanh_ready"], 1)

        def evacuate(q, J):
            act.wait_ge(sem["tile_used"], J * NT + (q * NI + 1) * NT)
            if not (q == 0 and isinstance(J, int) and J == 0):
                act.wait_ge(sem["rows_ready"],
                            {3: J * 2 + (NI + q * NI), LAST: J + (NI + q * NI + NI)}.get(q, J + (NI + q * NI)))
            func = ACT.Relu if q == 1 else ACT.Copy
            nc.scalar.activation(out_t[:, :], bank(J), func).then_inc(sem["out_t_ready"], 1)

        def operand_high(q, J):
            if q == 1:
                act.wait_ge(sem["rows_ready"], J + (NI + q * NI + 1))
                src = small[:, :]
            else:
                act.wait_ge(sem["rows_taken"], J + (NI + q * NI + 1))
                src = rows[:, :]
            nc.scalar.copy(group(v[(q + 1) % 2][0], J), src).then_inc(sem["v_high_ready"], 1)

        def norm(q, J):
            n = J + (NI if q == LAST else 0)
            act.wait_ge(sem["shift_ready"], n + 1)
            for c in range(RC):
                last = nc.scalar.activation(rows[:, chunk(c)], rows[:, chunk(c)], ACT.Identity,
                                            bias=shift[:, c:c + 1], scale=rstd[:, c:c + 1])
            last.then_inc(sem["norm_ready"], 1)

        def copy_x1t(J):
            act.wait_ge(sem["x1t_ready"], J + 1)
            nc.scalar.copy(x1_t[:, :], small2[:, :]).then_inc(sem["x1t_copied"], 1)

        def copy_h34(J):
            act.wait_ge(sem["h34_ready"], J + 1)
            nc.scalar.copy(kept_part(kept, J, H3), small[:, :]).then_inc(sem["h3_copied"], 1)
            nc.scalar.copy(kept_part(kept_r, J, H4_HIGH), small2[:, :]).then_inc(sem["h4_high_ready"], 1)

        def hf_high(J):
            act.wait_ge(sem["rows_ready"], (J + 1) * 2 + LAST * NI)
            nc.scalar.copy(group(v[0][0], J), small[:, :]).then_inc(sem["v_high_ready"], 1)

        def h3_split(I, parity):
            nc.scalar.copy(h3_high[:, bass.ds(parity * IB, IB)],
                           kept_part(kept, I, H3)).then_inc(sem["h3_high_ready"], 1)

        def epilogue(q, J, t, at):
            if t == at["evacuate"]:
                evacuate(q, J)
            if q < 3 and t == (at["take"] if q == 1 else at["split"]):
                operand_high(q, J)
            if q >= 3 and t == at["norm"]:
                norm(q, J)
            if q == 3 and t == at["x1t"]:
                copy_x1t(J)
            if q == 3 and t == at["project_out"]:
                copy_h34(J)
            if q == 3 and t == at["hf"]:
                hf_high(J)

        for t in range(NT):
            if t % TC == 0:
                g = t // TC
                act.wait_ge(sem["rows_ready"], g + 1)
                nc.scalar.copy(group(v[0][0], g), small[:, :]).then_inc(sem["v_high_ready"], 1)
            split_high(0, 0, t)
        for q in range(LAST):
            if q:
                for t in range(NT):
                    split_high(q, 0, t)
                    epilogue(q - 1, NI - 1, t, AHEAD)
            with act.Fori(0, NI - 1) as J:
                for t in range(NT):
                    split_high(q, J + 1, t)
                    epilogue(q, J, t, AHEAD)
        act.wait_ge(sem["h3_copied"], 1)
        h3_split(0, 0)
        act.wait_ge(sem["tile_used"], LAST * NI * NT)
        tanh_of(0, 0)
        for t in range(NT - 1):
            tanh_of(0, t + 1)
            split_high(LAST, 0, t)
            epilogue(3, NI - 1, t, CLOSE)
            if t == H3_SPLIT:
                act.wait_ge(sem["h3_copied"], 2)
                h3_split(1, 1)
        with act.Fori(0, NI - 1) as J:
            tanh_of(J + 1, 0)
            split_high(LAST, J, NT - 1)
            for t in range(NT - 1):
                tanh_of(J + 1, t + 1)
                split_high(LAST, J + 1, t)
                epilogue(LAST, J, t, CLOSE)
                if t == H3_SPLIT:
                    h3_split((J + 2) % NI, J % 2)
        split_high(LAST, NI - 1, NT - 1)
        evacuate(LAST, NI - 1)

    @block.vector
    def _(dve):
        def split_low(q, I, t):
            if t in pool_tiles(q):
                return
            dve.wait_ge(sem["high_ready"], I * NT + (q * NI * NT + t + 1))
            src = tanh_slot(t) if q == LAST else tile_in(t, I)
            nc.vector.tensor_tensor(split_slot(low, t), src, split_slot(high, t),
                                    ALU.subtract).then_inc(sem["low_ready"], 1)

        def signed(I, t):
            if t < NS:
                wait_tile_loaded(dve, I + LAST * NI, t)
            elif t == NS:
                dve.wait_ge(sem["late_loaded"], (I + (NI + 1)) * 16)
            dve.wait_ge(sem["tanh_ready"], I * NT + (t + 1))
            nc.vector.tensor_tensor(tanh_slot(t), tanh_slot(t), tile_in_last(t),
                                    ALU.mult).then_inc(sem["signed_ready"], 1)

        def scale_rows(q, J):
            dve.wait_ge(sem["rows_ready"], J + (NI + q * NI + 1))
            if not (q == 0 and isinstance(J, int) and J == 0):
                dve.wait_ge(sem["v_high_ready"], J + NI * (q + 1))
            f = filt[:, bass.ds(J * RC + (q // 2) * NI * RC, RC)]
            nc.vector.tensor_tensor(rows[:, :].rearrange("p (c d) -> p c d", c=RC),
                                    small[:, :].rearrange("p (c d) -> p c d", c=RC),
                                    f.rearrange("p (c o) -> p c o", o=1).to_broadcast([P, RC, D]),
                                    ALU.mult).then_inc(sem["rows_taken"], 1)

        def operand_low(q, J):
            dve.wait_ge(sem["v_high_ready"], J + (NI * (q + 1) + 1))
            if q in (0, 2):
                dve.wait_ge(sem["rows_taken"], J + (NI + q * NI + 1))
            src = small if q in (1, 3) else rows
            last = nc.vector.tensor_tensor(group(v[(q + 1) % 2][1], J), src[:, :],
                                           group(v[(q + 1) % 2][0], J), ALU.subtract)
            last.then_inc(sem["v_low_ready"], 1)
            if q == 1:
                dve.wait_ge(sem["v_low_ready"], J + (NI * (q + 1) + 1))
                dve.sem_inc(sem["rows_taken"], 1)

        def add_residual(q, J):
            if q == LAST:
                dve.wait_ge(sem["rows_ready"], J + (NI + q * NI + NI + 1))
                dve.wait_ge(sem["residual_ready"], NI + 1)
                dve.wait_ge(sem["stored"], (J + 1) * 16)
            else:
                dve.wait_ge(sem["rows_ready"], J * 2 + (NI + q * NI + 1))
                dve.wait_ge(sem["x_loaded"], (J + 1) * 16)
                dve.wait_ge(sem["residual_ready"], J + 1)
            nc.vector.tensor_tensor(rows[:, :], small[:, :], kept_part(kept, J, RESIDUAL),
                                    ALU.add).then_inc(sem["rows_taken"], 1)

        def row_stats(q, J):
            dve.wait_ge(sem["rows_taken"], J + (NI + q * NI + 1))
            for c in range(RC):
                last = nc.vector.bn_stats(stats[:, c * 6:(c + 1) * 6], rows[:, chunk(c)])
            last.then_inc(sem["stats_ready"], 1)

        def row_moments(q, J):
            n = J + (NI if q == LAST else 0)
            dve.wait_ge(sem["stats_ready"], n + 1)
            dve.sem_inc(sem["stats_seen"], 1)
            for c in range(RC):
                last = nc.vector.bn_aggr(moments[:, c * 2:(c + 1) * 2], stats[:, c * 6:(c + 1) * 6])
            last.then_inc(sem["moments_ready"], 1)
            dve.wait_ge(sem["moments_ready"], n + 1)
            nc.vector.tensor_scalar(variance[:, :].rearrange("p (c o) -> p c o", o=1),
                                    moments[:, :].rearrange("p (c o) -> p c o", o=2)[:, :, 1:2],
                                    EPS, None, ALU.add).then_inc(sem["variance_ready"], 1)

        def norm_last():
            dve.wait_ge(sem["rstd_ready"], 2 * NI)
            for c in range(RC):
                last = nc.vector.tensor_scalar(rows[:, chunk(c)], rows[:, chunk(c)],
                                               moments[:, c * 2:c * 2 + 1], rstd[:, c:c + 1],
                                               ALU.subtract, ALU.mult)
            last.then_inc(sem["last_norm_ready"], 1)

        def h4_low(J):
            dve.wait_ge(sem["h4_high_ready"], J + 1)
            nc.vector.tensor_tensor(kept_part(kept_r, J, H4_LOW), small2[:, :],
                                    kept_part(kept_r, J, H4_HIGH),
                                    ALU.subtract).then_inc(sem["h4_low_ready"], 1)

        def epilogue(q, J, t, at):
            if q in (0, 2) and t == at["take"]:
                scale_rows(q, J)
            if q in (0, 2) and t == at["split_low"]:
                operand_low(q, J)
            if q == 1 and t == at["split"]:
                operand_low(q, J)
            if q >= 3 and t == at["take"]:
                add_residual(q, J)
            if q >= 3 and t == at["stats"]:
                row_stats(q, J)
            if q >= 3 and t == at["moments"]:
                row_moments(q, J)
            if q == 3 and t == at["h4_low"]:
                h4_low(J)
            if q == 3 and t == at["hf_low"]:
                operand_low(q, J)

        for t in range(NT):
            if t % TC == 0:
                g = t // TC
                dve.wait_ge(sem["v_high_ready"], g + 1)
                nc.vector.tensor_tensor(group(v[0][1], g), small[:, :], group(v[0][0], g),
                                        ALU.subtract).then_inc(sem["v_low_ready"], 1)
            split_low(0, 0, t)
        dve.wait_ge(sem["v_low_ready"], NI)
        dve.sem_inc(sem["rows_taken"], NI)
        for q in range(LAST):
            if q:
                for t in range(NT):
                    split_low(q, 0, t)
                    epilogue(q - 1, NI - 1, t, AHEAD)
            with dve.Fori(0, NI - 1) as J:
                for t in range(NT):
                    split_low(q, J + 1, t)
                    epilogue(q, J, t, AHEAD)
        signed(0, 0)
        for t in range(NT - 1):
            signed(0, t + 1)
            split_low(LAST, 0, t)
            epilogue(3, NI - 1, t, CLOSE)
        with dve.Fori(0, NI - 1) as J:
            signed(J + 1, 0)
            split_low(LAST, J, NT - 1)
            for t in range(NT - 1):
                signed(J + 1, t + 1)
                split_low(LAST, J + 1, t)
                epilogue(LAST, J, t, CLOSE)
        split_low(LAST, NI - 1, NT - 1)
        add_residual(LAST, NI - 1)
        row_stats(LAST, NI - 1)
        row_moments(LAST, NI - 1)
        norm_last()

    @block.gpsimd
    def _(pool):
        def split_low(q, I, t):
            pool.wait_ge(sem["high_ready"], I * NT + (q * NI * NT + t + 1))
            src = tanh_slot(t) if q == LAST else tile_in(t, I)
            nc.gpsimd.tensor_tensor(split_slot(low, t), src, split_slot(high, t),
                                    ALU.subtract).then_inc(sem["pool_low_ready"], 1)

        def inverse_deviation(n):
            pool.wait_ge(sem["variance_ready"], n)
            nc.gpsimd.tensor_tensor(rstd[:, :], variance[:, :], power[:, :],
                                    ALU.pow).then_inc(sem["rstd_ready"], 1)

        def minus_mean():
            means = moments[:, :].rearrange("p (c o) -> p c o", o=2)[:, :, 0:1]
            nc.gpsimd.tensor_tensor(shift[:, :].rearrange("p (c o) -> p c o", o=1), means,
                                    minus[:, :].rearrange("p (c o) -> p c o", o=1),
                                    ALU.mult).then_inc(sem["minus_ready"], 1)

        def shift_of(n):
            inverse_deviation(n)
            minus_mean()
            pool.wait_ge(sem["rstd_ready"], n)
            pool.wait_ge(sem["minus_ready"], n)
            nc.gpsimd.tensor_tensor(shift[:, :], shift[:, :], rstd[:, :],
                                    ALU.mult).then_inc(sem["shift_ready"], 1)

        def h3_split(I, parity, count):
            pool.wait_ge(sem["h3_high_ready"], count)
            nc.gpsimd.tensor_tensor(h3_low[:, bass.ds(parity * IB, IB)], kept_part(kept, I, H3),
                                    h3_high[:, bass.ds(parity * IB, IB)],
                                    ALU.subtract).then_inc(sem["h3_low_ready"], 1)

        def residual(J):
            pool.wait_ge(sem["v_low_ready"], J + (LAST * NI + 1))
            place = kept_part(kept, J, RESIDUAL)
            nc.gpsimd.tensor_tensor(place, rows[:, :], group(v[0][0], J),
                                    ALU.add).then_inc(sem["partial_ready"], 1)
            pool.wait_ge(sem["partial_ready"], J + 1)
            nc.gpsimd.tensor_tensor(place, place, group(v[0][1], J),
                                    ALU.add).then_inc(sem["residual_ready"], 1)

        nc.gpsimd.memset(power[:, :], -0.5).then_inc(sem["power_ready"], 1)
        nc.gpsimd.memset(minus[:, :], -1.0).then_inc(sem["power_ready"], 1)
        pool.wait_ge(sem["power_ready"], 2)
        pool.sem_inc(sem["residual_ready"], 1)
        for t in pool_tiles(3):
            split_low(3, 0, t)
        with pool.Fori(0, NI - 1) as J:
            split_low(3, J + 1, POOL_TILES[0])
            shift_of(J + 1)
            split_low(3, J + 1, POOL_TILES[1])
            residual(J)
        h3_split(0, 0, 1)
        shift_of(NI)
        h3_split(1, 1, 2)
        residual(NI - 1)
        with pool.Fori(0, NI - 1) as J:
            shift_of(J + (NI + 1))
            h3_split((J + 2) % NI, J % 2, J + 3)
        inverse_deviation(2 * NI)

    block.__exit__(None, None, None)


def kernel(x, adj, L0_gnn_W1, L0_gnn_f1, L0_gnn_W2, L0_gnn_f2, L1_gnn_W1, L1_gnn_W2, L1_gnn_Wf):
    import concourse.bacc as bacc
    from concourse.bass_utils import run_bass_kernel_spmd

    x, adj = np.asarray(x), np.asarray(adj)
    tiles = adj.reshape(NI, IB, NT, TC, P).transpose(0, 2, 4, 3, 1).reshape(NI * NT * P, TW)
    arrays = {
        "adj": tiles,
        "x_rows": x.reshape(NI, RC, P, D).transpose(0, 2, 1, 3).reshape(NI * P, IB),
        "x_cols": x.T,
        "weights": np.concatenate([np.asarray(L0_gnn_W1), np.asarray(L0_gnn_W2), np.asarray(L1_gnn_W1).T,
                                   np.asarray(L1_gnn_W2).T, np.asarray(L1_gnn_Wf).T], axis=1),
        "filters": np.concatenate([np.asarray(f).reshape(N // P, P).T for f in (L0_gnn_f1, L0_gnn_f2)], axis=1),
        "identity": np.eye(P, dtype=np.float32),
    }
    arrays = {k: np.ascontiguousarray(a) for k, a in arrays.items()}
    nc = bacc.Bacc("TRN2", target_bir_lowering=False, num_devices=1)
    handles = {k: nc.dram_tensor(k, a.shape, F32, kind="ExternalInput").ap() for k, a in arrays.items()}
    out = nc.dram_tensor("out", (NI * P, IB), F32, kind="ExternalOutput").ap()
    build(nc, handles["adj"], handles["x_rows"], handles["x_cols"], handles["weights"],
          handles["filters"], handles["identity"], out)
    result = run_bass_kernel_spmd(nc, [arrays], core_ids=[0])
    got = result.results[0]["out"]
    return got.reshape(NI, P, RC, D).transpose(0, 2, 1, 3).reshape(N, D)
```

```python
import numpy as np
import concourse.bass as bass
import concourse.mybir as mybir

F32 = mybir.dt.float32
F32R = mybir.dt.float32r
ALU = mybir.AluOpType
ACT = mybir.ActivationFunctionType

P = 128
N = 4096
D = 128
IB = 512
NI = N // IB
RC = IB // P
TC = 2
TW = TC * IB
NT = N // (TC * P)
KEPT = 2
NS = NT - KEPT
LEAD = 3
RING = 7
SPLITS = 4
TANHS = 4
POOL_PASS = 3
POOL_STEPS = (5, 11)
LAST = 4
SHORT = 4
NSHORT = NT // 2
EPS = 1e-5


def build(nc, adj, x_rows, x_cols, weights, filters, identity, out):
    base = nc.sbuf_base
    place = [(base + 31) // 32 * 32]

    def sb(name, free, dtype, at=None):
        if at is None:
            at = place[0]
            place[0] += -(-free * 4 // 32) * 32
        return nc.alloc_sbuf_tensor_at(name, [P, free], dtype, offset=at), at

    v = [[None, None], [None, None]]
    v[0][0], _ = sb("v_even_high", N, F32R)
    v[0][1], _ = sb("v_even_low", N, F32R)
    v[1][0], odd_at = sb("v_odd_high", N, F32R)
    v[1][1], odd_low_at = sb("v_odd_low", N, F32R)
    x_t, _ = sb("x_t", N, F32, odd_at)
    tanh_tiles, _ = sb("tanh_tiles", TANHS * TW, F32, odd_at)
    late_tiles, _ = sb("late_tiles", KEPT * TW, F32, odd_low_at)
    kept, kept_at = sb("kept", NI * KEPT * TW, F32)
    kept_r, _ = sb("kept_r", NI * KEPT * TW, F32R, kept_at)
    KB = KEPT * TW
    H4_HIGH, H4_LOW, H3, RESIDUAL = 0, IB, 2 * IB, 3 * IB
    ring, _ = sb("ring", RING * TW, F32)
    high, _ = sb("high", SPLITS * TW, F32R)
    low, _ = sb("low", SPLITS * TW, F32R)
    h3_high, _ = sb("h3_high", 2 * IB, F32R)
    h3_low, _ = sb("h3_low", 2 * IB, F32R)
    out_t, _ = sb("out_t", IB, F32)
    rows, _ = sb("rows", IB, F32)
    x1_t, _ = sb("x1_t", IB, F32)
    w, _ = sb("w", 5 * D, F32)
    filt, _ = sb("filt", 2 * NI * RC, F32)
    ident, _ = sb("ident", P, F32)
    stats, _ = sb("stats", RC * 6, F32)
    moments, _ = sb("moments", RC * 2, F32)
    variance, _ = sb("variance", RC, F32)
    rstd, _ = sb("rstd", RC, F32)
    power, _ = sb("power", RC, F32)
    minus, _ = sb("minus", RC, F32)
    shift, _ = sb("shift", RC, F32)
    assert place[0] <= nc.sbuf_usable_end, (place[0], nc.sbuf_usable_end)

    acc = nc.alloc_psum_tensor("acc", [P, 2 * IB], F32)
    score = nc.alloc_psum_tensor("score", [P, 2 * TW], F32)
    small = nc.alloc_psum_tensor("small", [P, IB], F32)
    small2 = nc.alloc_psum_tensor("small2", [P, IB], F32)

    sem = {}
    for name in (
        "weights_loaded", "late_loaded", "x_loaded", "stored",
        "tile_used", "rows_ready", "x1t_ready", "h34_ready", "score_ready",
        "high_ready", "out_t_ready", "v_high_ready", "x1t_copied", "h3_copied", "h4_high_ready",
        "h3_high_ready", "tanh_ready", "norm_ready",
        "low_ready", "rows_taken", "v_low_ready", "stats_ready", "stats_seen", "moments_ready", "variance_ready",
        "h4_low_ready", "signed_ready", "last_norm_ready",
        "power_ready", "pool_low_ready", "rstd_ready", "partial_ready", "residual_ready", "h3_low_ready", "shift_ready", "minus_ready",
    ):
        sem[name] = nc.alloc_semaphore(name)
    ring_loaded = [nc.alloc_semaphore(f"ring_loaded{s}") for s in range(RING)]
    xt_loaded = [nc.alloc_semaphore(f"xt_loaded{g}") for g in range(NI)]

    HALF = NT // 2
    STREAMED = [*range(1, HALF - 2), HALF, HALF + 1, HALF - 2, HALF - 1, *range(HALF + 2, NT - 1)]

    def tile_at(n, short=False):
        if short:
            return NT - NSHORT + n
        return STREAMED[n] if n < NS else (0, NT - 1)[n - NS]

    def place_of(tile):
        return {0: 0, NT - 1: 1}.get(tile, tile + 1)

    GROUP_ORDER = list(dict.fromkeys(tile_at(n) * TC // RC for n in range(NT)))
    GROUP_STEPS = [min(n for n in range(NT) if tile_at(n) * TC // RC == g) for g in GROUP_ORDER]
    EARLY_STEPS = tuple(n for n in range(NT) if tile_at(n) not in [tile_at(k, True) for k in range(NSHORT)])
    EARLY_GROUPS = max(tile_at(n) for n in EARLY_STEPS) * TC // RC + 1
    LAST_GROUP_STEP = [n for n in EARLY_STEPS if tile_at(n) * TC // RC == EARLY_GROUPS - 1][0]

    def tile_in(n, block, short=False):
        if n < (NSHORT - 1 if short else NS):
            return ring[:, (n % RING) * TW:(n % RING + 1) * TW]
        return kept[:, bass.ds(block * KB + place_of(tile_at(n, short)) * TW, TW)]

    def tile_in_last(t):
        if t < NS:
            return ring[:, (t % RING) * TW:(t % RING + 1) * TW]
        return late_tiles[:, (NT - 1 - t) * TW:(NT - t) * TW]

    def split_slot(buffer, t):
        return buffer[:, (t % SPLITS) * TW:(t % SPLITS + 1) * TW]

    def tanh_slot(t):
        return tanh_tiles[:, (t % TANHS) * TW:(t % TANHS + 1) * TW]

    def bank(block):
        return acc[:, bass.ds((block % 2) * IB, IB)]

    def early_bank(block):
        return score[:, bass.ds(block * IB - SHORT * IB, IB)]

    def group(buffer, g):
        return buffer[:, bass.ds(g * IB, IB)]

    def kept_part(buffer, block, part):
        return buffer[:, bass.ds(block * KB + part, IB)]

    def chunk(c):
        return slice(c * D, (c + 1) * D)

    def weight(k):
        return w[:, k * D:(k + 1) * D]

    W1, W2, W3, W4, WF = range(5)

    def tiles_before(q, I, short=False):
        if short:
            return I * NSHORT + (NI * NT + SHORT * (NT - NSHORT))
        return I * NT + (q * NI * NT - (NI - SHORT) * (NT - NSHORT) * (q > 1))

    def wait_tile_loaded(eng, q, I, n, short=False):
        if short:
            fills = I + (NI * 2 + SHORT + 1)
        else:
            fills = I * 2 + (q * NI * 2 - (NI - SHORT) * (q > 1) + n // RING + 1)
        eng.wait_ge(ring_loaded[n % RING], fills * 16)

    def pool_steps(q):
        return POOL_STEPS if q == POOL_PASS else ()

    def wait_low(eng, q, I, n, short=False):
        if n < 0 and not short:
            I, n = I - 1, n + NT
            if isinstance(I, int) and I < 0:
                q, I = q - 1, NI - 1
        helped = pool_steps(q)
        if n in helped:
            eng.wait_ge(sem["pool_low_ready"], I * len(helped) + (helped.index(n) + 1))
        else:
            if short:
                before = tiles_before(q, I, True)
            else:
                before = I * (NT - len(helped)) + (tiles_before(q, 0) - NI * len(POOL_STEPS) * (q > POOL_PASS))
            eng.wait_ge(sem["low_ready"], before + (n + 1 - sum(k <= n for k in helped)))

    AHEAD = dict(evacuate=3, transpose=1, take=5, split=6, split_low=7, add=4, stats=5, moments=6,
                 norm=9, transpose2=8, x1t=10, project=9, project_out=12, project2=11, h4_low=13,
                 hf=14, hf_low=15)
    CLOSE = dict(evacuate=1, transpose=2, add=4, stats=5, moments=6, norm=9)
    FIRST = dict(evacuate=-1, transpose=-1, add=-1, stats=3, moments=4, norm=6, transpose2=6, x1t=8,
                 project=8, project_out=9, project2=9, h4_low=10, hf=10, hf_low=10)
    H3_SPLIT = 10

    block = nc.Block()
    block.__enter__()

    @block.sync
    def _(sp):
        def load_tile(row, n, tile):
            nc.sync.dma_start(ring[:, (n % RING) * TW:(n % RING + 1) * TW],
                              adj[bass.ds((row * NT + place_of(tile)) * P, P), :]).then_inc(ring_loaded[n % RING], 16)

        def wait_slot(q, I, n, short=False):
            if short:
                wait_low(sp, q, I, n - NSHORT, True)
            elif q == 2 and isinstance(I, int) and n < RING:
                wait_low(sp, 1, NI - 1, n, True)
            else:
                wait_low(sp, q, I, n - RING if n >= RING else n - RING - KEPT)

        def load_pair(buffer, offset, row, first, last):
            dst = buffer[:, bass.ds(offset, KB)].rearrange("p (t n) -> p t n", t=KEPT)
            places = adj[bass.ds((row * NT + first) * P, (last - first + 1) * P), :]
            src = places.rearrange("(t p) n -> p t n", p=P)[:, ::last - first, :]
            nc.sync.dma_start(dst, src).then_inc(sem["late_loaded"], 16)

        def load_x(I):
            nc.sync.dma_start(kept_part(kept, I, RESIDUAL),
                              x_rows[bass.ds(I * P, P), :]).then_inc(sem["x_loaded"], 16)

        def store_rows(J):
            sp.wait_ge(sem["norm_ready"], NI + J + 1)
            nc.sync.dma_start(out[bass.ds(J * P, P), :], rows[:, :]).then_inc(sem["stored"], 16)

        sp.sem_inc(sem["stored"], 16)
        nc.sync.dma_start(w[:, :], weights[:, :]).then_inc(sem["weights_loaded"], 16)
        nc.sync.dma_start(filt[:, :], filters[:, :]).then_inc(sem["weights_loaded"], 16)
        nc.sync.dma_start(ident[:, :], identity[:, :]).then_inc(sem["weights_loaded"], 16)

        def load_x_t(g):
            nc.sync.dma_start(x_t[:, g * IB:(g + 1) * IB],
                              x_cols[:, g * IB:(g + 1) * IB]).then_inc(xt_loaded[g], 16)

        load_x_t(GROUP_ORDER[0])
        for n in range(NS):
            if n >= RING:
                wait_slot(0, 0, n)
            load_tile(0, n, tile_at(n))
            if n + 1 < NI:
                load_x_t(GROUP_ORDER[n + 1])
            if n == RING:
                load_pair(kept, 0, 0, 0, 1)
        with sp.Fori(1, NI) as I:
            for n in range(NS):
                wait_slot(0, I, n)
                load_tile(I, n, tile_at(n))
                if n == RING:
                    sp.wait_ge(sem["late_loaded"], I * 16)
                    load_pair(kept, I * KB, I, 0, 1)
        for q in range(1, LAST):
            for n in range(NS):
                wait_slot(q, 0, n)
                load_tile(0, n, tile_at(n))
            with sp.Fori(1, SHORT if q == 1 else NI) as I:
                for n in range(NS):
                    wait_slot(q, I, n)
                    load_tile(I, n, tile_at(n))
                    if q == 3 and n == RING:
                        wait_low(sp, 3, I, -1)
                        load_x(I - 1)
            if q == 1:
                with sp.Fori(SHORT, NI) as I:
                    for n in range(NSHORT - 1):
                        wait_slot(q, I, n, True)
                        load_tile(I, n, tile_at(n, True))
        for n in range(NS):
            if n >= RING:
                sp.wait_ge(sem["signed_ready"], n - RING + 1)
            else:
                wait_slot(LAST, 0, n)
            load_tile(0, n, n)
            if n == RING - 1:
                wait_low(sp, LAST, 0, -1)
                load_x(NI - 1)
            if n == RING + 1:
                sp.wait_ge(sem["tile_used"], tiles_before(LAST, 0))
                load_pair(late_tiles, 0, 0, 1, NT - 1)
        with sp.Fori(1, NI) as I:
            for n in range(NS):
                sp.wait_ge(sem["signed_ready"],
                           I * NT + (n - RING + 1 if n >= RING else n - RING + 1 - KEPT))
                load_tile(I, n, n)
                if n == RING + 1:
                    sp.wait_ge(sem["signed_ready"], I * NT)
                    load_pair(late_tiles, 0, I, 1, NT - 1)
                if n == NS - 2:
                    store_rows(I - 1)
        sp.wait_ge(sem["last_norm_ready"], 1)
        nc.sync.dma_start(out[(NI - 1) * P:NI * P, :], rows[:, :]).then_inc(sem["stored"], 16)
        sp.wait_ge(sem["stored"], (NI + 1) * 16)

    @block.tensor
    def _(pe):
        def project_x(k):
            g = GROUP_ORDER[k]
            pe.wait_ge(xt_loaded[g], 16)
            if k:
                pe.wait_ge(sem["v_low_ready"], k)
            for c in range(RC):
                last = nc.tensor.matmul(small[:, chunk(c)], lhsT=x_t[:, g * IB + c * P:g * IB + (c + 1) * P],
                                        rhs=weight(W1), start=True, stop=True)
            last.then_inc(sem["rows_ready"], 1)

        def add_tile(operand, total, n, tile, begin, end):
            for c in range(TC):
                J = tile * TC + c
                v_high, v_low = (v[operand][half][:, J * D:(J + 1) * D] for half in (0, 1))
                a_high, a_low = (split_slot(buf, n)[:, c * IB:(c + 1) * IB] for buf in (high, low))
                nc.tensor.matmul(total, lhsT=v_high, rhs=a_high, start=begin and c == 0, stop=False)
                nc.tensor.matmul(total, lhsT=v_high, rhs=a_low, start=False, stop=False)
                last = nc.tensor.matmul(total, lhsT=v_low, rhs=a_high, start=False,
                                        stop=end and c == TC - 1)
            return last

        def product(q, I, n):
            wait_low(pe, q, I, n)
            tile = n if q == LAST else tile_at(n)
            last = add_tile(q % 2, bank(I), n, tile, n == 0, n == NT - 1)
            last.then_inc(sem["tile_used"], 1)

        def product_and_early(I, n):
            wait_low(pe, 0, I, n)
            last = add_tile(0, bank(I), n, tile_at(n), n == 0, n == NT - 1)
            if n in EARLY_STEPS:
                last = add_tile(1, early_bank(I), n, tile_at(n), n == 0, False)
            last.then_inc(sem["tile_used"], 1)

        def short_product(I, n):
            wait_low(pe, 1, I, n, True)
            last = add_tile(1, early_bank(I), n, tile_at(n, True), False, n == NSHORT - 1)
            last.then_inc(sem["tile_used"], 1)

        def transposed_rows(q, J):
            pe.wait_ge(sem["out_t_ready"], J + (q * NI + 1))
            if q < LAST:
                pe.wait_ge(sem["rows_taken"], J + NI * (q + 1))
            if q == 3:
                if not (isinstance(J, int) and J == 0):
                    pe.wait_ge(sem["v_low_ready"], J + NI * LAST)
            if q == LAST:
                pe.wait_ge(sem["rows_taken"], J + NI * (q + 1))
                pe.wait_ge(sem["v_low_ready"], NI * (LAST + 1))
            for c in range(RC):
                if q == 1:
                    last = nc.tensor.matmul(small[:, chunk(c)], lhsT=out_t[:, c * P:(c + 1) * P],
                                            rhs=weight(W2), start=True, stop=True)
                else:
                    last = nc.tensor.transpose(small[:, chunk(c)], out_t[:, c * P:(c + 1) * P], ident[:, :])
            last.then_inc(sem["rows_ready"], 1)

        def transposed_x1(J):
            pe.wait_ge(sem["norm_ready"], J + 1)
            for c in range(RC):
                last = nc.tensor.transpose(small2[:, c * P:(c + 1) * P], rows[:, chunk(c)], ident[:, :])
            last.then_inc(sem["x1t_ready"], 1)

        def scores_operands(J):
            pe.wait_ge(sem["x1t_copied"], J + 1)
            nc.tensor.matmul(small[:, :], lhsT=weight(W3), rhs=x1_t[:, :], start=True, stop=True)
            nc.tensor.matmul(small2[:, :], lhsT=weight(W4), rhs=x1_t[:, :],
                             start=True, stop=True).then_inc(sem["h34_ready"], 1)

        def value_rows(J):
            pe.wait_ge(sem["h3_copied"], J + 1)
            for c in range(RC):
                last = nc.tensor.matmul(small[:, chunk(c)], lhsT=x1_t[:, c * P:(c + 1) * P],
                                        rhs=weight(WF), start=True, stop=True)
            last.then_inc(sem["rows_ready"], 1)

        def epilogue(q, J, t, at):
            if t == at["transpose"]:
                transposed_rows(q, J)
            if q == 3 and t == at["transpose2"]:
                transposed_x1(J)
            if q == 3 and t == at["project"]:
                scores_operands(J)
            if q == 3 and t == at["project2"]:
                value_rows(J)

        def scores(I, t):
            if not (isinstance(I, int) and I == 0 and t < 2):
                pe.wait_ge(sem["tanh_ready"], I * NT + (t - 1))
            for c in range(TC):
                J = t * TC + c
                g, r = J // RC, J % RC
                at = g * KB + r * P
                h4_high = kept_r[:, at + H4_HIGH:at + H4_HIGH + P]
                h4_low = kept_r[:, at + H4_LOW:at + H4_LOW + P]
                z = score[:, (t % 2) * TW + c * IB:(t % 2) * TW + (c + 1) * IB]
                b_high, b_low = (buf[:, bass.ds((I % 2) * IB, IB)] for buf in (h3_high, h3_low))
                nc.tensor.matmul(z, lhsT=h4_high, rhs=b_high, start=True, stop=False)
                nc.tensor.matmul(z, lhsT=h4_high, rhs=b_low, start=False, stop=False)
                last = nc.tensor.matmul(z, lhsT=h4_low, rhs=b_high, start=False, stop=True)
            last.then_inc(sem["score_ready"], 1)

        pe.wait_ge(sem["weights_loaded"], 3 * 16)
        project_x(0)
        for n in range(NT):
            if n in GROUP_STEPS:
                k = GROUP_STEPS.index(n)
                if k + 1 < NI:
                    project_x(k + 1)
                pe.wait_ge(sem["v_low_ready"], k + 1)
            product(0, 0, n)
        with pe.Fori(0, SHORT - 1) as J:
            for n in range(NT):
                product(0, J + 1, n)
                epilogue(0, J, n, AHEAD)
        pe.wait_ge(sem["v_low_ready"], NI + EARLY_GROUPS - 1)
        with pe.Fori(SHORT - 1, NI - 1) as J:
            for n in range(NT):
                if n == LAST_GROUP_STEP:
                    pe.wait_ge(sem["v_low_ready"], NI + EARLY_GROUPS)
                product_and_early(J + 1, n)
                epilogue(0, J, n, AHEAD)
        for q in range(1, LAST):
            for n in range(NT):
                if n in GROUP_STEPS:
                    pe.wait_ge(sem["v_low_ready"], q * NI + tile_at(n) * TC // RC + 1)
                product(q, 0, n)
                epilogue(q - 1, NI - 1, n, AHEAD)
            with pe.Fori(0, (SHORT if q == 1 else NI) - 1) as J:
                for n in range(NT):
                    product(q, J + 1, n)
                    epilogue(q, J, n, AHEAD)
            if q == 1:
                with pe.Fori(SHORT - 1, NI - 1) as J:
                    for n in range(NSHORT):
                        short_product(J + 1, n)
                        epilogue(q, J, n, AHEAD)

        pe.wait_ge(sem["h3_low_ready"], 1)
        for t in range(LEAD):
            scores(0, t)
            if t == 0:
                epilogue(3, NI - 1, -1, FIRST)
        for t in range(NT - LEAD):
            if (t + LEAD) % TC == 0:
                pe.wait_ge(sem["h4_low_ready"], (t + LEAD) // TC + 1)
            scores(0, t + LEAD)
            if t % TC == 0:
                pe.wait_ge(sem["v_low_ready"], LAST * NI + t // TC + 1)
            product(LAST, 0, t)
            epilogue(3, NI - 1, t, FIRST)
        with pe.Fori(0, NI - 1) as J:
            pe.wait_ge(sem["h3_low_ready"], J + 2)
            pe.wait_ge(sem["v_low_ready"], (LAST + 1) * NI)
            for t in range(LEAD):
                scores(J + 1, t)
                product(LAST, J, NT - LEAD + t)
            for t in range(NT - LEAD):
                scores(J + 1, t + LEAD)
                product(LAST, J + 1, t)
                epilogue(LAST, J, t, CLOSE)
        for t in range(NT - LEAD, NT):
            product(LAST, NI - 1, t)
        transposed_rows(LAST, NI - 1)

    @block.scalar
    def _(act):
        def split_high(q, I, n, short=False):
            if q == LAST:
                act.wait_ge(sem["signed_ready"], I * NT + (n + 1))
                src = tanh_slot(n)
            else:
                if n < (NSHORT - 1 if short else NS):
                    wait_tile_loaded(act, q, I, n, short)
                elif q == 0 and n == NS:
                    act.wait_ge(sem["late_loaded"], (I + 1) * 16)
                src = tile_in(n, I, short)
            if not (q == 0 and isinstance(I, int) and n < SPLITS):
                act.wait_ge(sem["tile_used"],
                            tiles_before(q, I, short) + (n + 1 - SPLITS))
            nc.scalar.copy(split_slot(high, n), src).then_inc(sem["high_ready"], 1)

        def tanh_of(I, t):
            act.wait_ge(sem["score_ready"], I * NT + (t + 1))
            if not (isinstance(I, int) and I == 0 and t < TANHS):
                wait_low(act, LAST, I, t - TANHS)
            nc.scalar.activation(tanh_slot(t), score[:, (t % 2) * TW:(t % 2 + 1) * TW], ACT.Tanh,
                                 scale=-0.5).then_inc(sem["tanh_ready"], 1)

        def evacuate(q, J, short=False):
            act.wait_ge(sem["tile_used"], tiles_before(q, J, short) + (NSHORT if short else NT))
            if not (q == 0 and isinstance(J, int) and J == 0):
                act.wait_ge(sem["rows_ready"],
                            {3: J * 2 + (NI + q * NI), LAST: J + (NI + q * NI + NI)}.get(q, J + (NI + q * NI)))
            func = ACT.Relu if q == 1 else ACT.Copy
            nc.scalar.activation(out_t[:, :], early_bank(J) if short else bank(J), func).then_inc(sem["out_t_ready"], 1)

        def operand_high(q, J):
            if q == 1:
                act.wait_ge(sem["rows_ready"], J + (NI + q * NI + 1))
                src = small[:, :]
            else:
                act.wait_ge(sem["rows_taken"], J + (NI + q * NI + 1))
                src = rows[:, :]
            nc.scalar.copy(group(v[(q + 1) % 2][0], J), src).then_inc(sem["v_high_ready"], 1)

        def norm(q, J):
            n = J + (NI if q == LAST else 0)
            act.wait_ge(sem["shift_ready"], n + 1)
            for c in range(RC):
                last = nc.scalar.activation(rows[:, chunk(c)], rows[:, chunk(c)], ACT.Identity,
                                            bias=shift[:, c:c + 1], scale=rstd[:, c:c + 1])
            last.then_inc(sem["norm_ready"], 1)

        def copy_x1t(J):
            act.wait_ge(sem["x1t_ready"], J + 1)
            nc.scalar.copy(x1_t[:, :], small2[:, :]).then_inc(sem["x1t_copied"], 1)

        def copy_h34(J):
            act.wait_ge(sem["h34_ready"], J + 1)
            nc.scalar.copy(kept_part(kept, J, H3), small[:, :]).then_inc(sem["h3_copied"], 1)
            nc.scalar.copy(kept_part(kept_r, J, H4_HIGH), small2[:, :]).then_inc(sem["h4_high_ready"], 1)

        def hf_high(J):
            act.wait_ge(sem["rows_ready"], (J + 1) * 2 + LAST * NI)
            nc.scalar.copy(group(v[0][0], J), small[:, :]).then_inc(sem["v_high_ready"], 1)

        def h3_split(I, parity):
            nc.scalar.copy(h3_high[:, bass.ds(parity * IB, IB)],
                           kept_part(kept, I, H3)).then_inc(sem["h3_high_ready"], 1)

        def epilogue(q, J, t, at, short=False):
            if t == at["evacuate"]:
                evacuate(q, J, short)
            if q < 3 and t == (at["take"] if q == 1 else at["split"]):
                operand_high(q, J)
            if q >= 3 and t == at["norm"]:
                norm(q, J)
            if q == 3 and t == at["x1t"]:
                copy_x1t(J)
            if q == 3 and t == at["project_out"]:
                copy_h34(J)
            if q == 3 and t == at["hf"]:
                hf_high(J)

        for n in range(NT):
            if n in GROUP_STEPS:
                k = GROUP_STEPS.index(n)
                act.wait_ge(sem["rows_ready"], k + 1)
                nc.scalar.copy(group(v[0][0], GROUP_ORDER[k]), small[:, :]).then_inc(
                    sem["v_high_ready"], 1)
            split_high(0, 0, n)
        for q in range(LAST):
            if q:
                for n in range(NT):
                    split_high(q, 0, n)
                    epilogue(q - 1, NI - 1, n, AHEAD, q == 2)
            with act.Fori(0, (SHORT if q == 1 else NI) - 1) as J:
                for n in range(NT):
                    split_high(q, J + 1, n)
                    epilogue(q, J, n, AHEAD)
            if q == 1:
                for J in range(SHORT - 1, NI - 1):
                    for n in range(NSHORT):
                        split_high(q, J + 1, n, True)
                        epilogue(q, J, n, AHEAD, J >= SHORT)
        act.wait_ge(sem["h3_copied"], 1)
        h3_split(0, 0)
        act.wait_ge(sem["tile_used"], tiles_before(LAST, 0))
        epilogue(3, NI - 1, -1, FIRST)
        tanh_of(0, 0)
        for t in range(NT - 1):
            tanh_of(0, t + 1)
            split_high(LAST, 0, t)
            epilogue(3, NI - 1, t, FIRST)
            if t == H3_SPLIT:
                act.wait_ge(sem["h3_copied"], 2)
                h3_split(1, 1)
        with act.Fori(0, NI - 1) as J:
            tanh_of(J + 1, 0)
            split_high(LAST, J, NT - 1)
            for t in range(NT - 1):
                tanh_of(J + 1, t + 1)
                split_high(LAST, J + 1, t)
                epilogue(LAST, J, t, CLOSE)
                if t == H3_SPLIT:
                    h3_split((J + 2) % NI, J % 2)
        split_high(LAST, NI - 1, NT - 1)
        evacuate(LAST, NI - 1)

    @block.vector
    def _(dve):
        def split_low(q, I, n, short=False):
            if n in pool_steps(q):
                return
            dve.wait_ge(sem["high_ready"], tiles_before(q, I, short) + (n + 1))
            src = tanh_slot(n) if q == LAST else tile_in(n, I, short)
            nc.vector.tensor_tensor(split_slot(low, n), src, split_slot(high, n),
                                    ALU.subtract).then_inc(sem["low_ready"], 1)

        def signed(I, t):
            if t < NS:
                wait_tile_loaded(dve, LAST, I, t)
            elif t == NS:
                dve.wait_ge(sem["late_loaded"], (I + (NI + 1)) * 16)
            dve.wait_ge(sem["tanh_ready"], I * NT + (t + 1))
            nc.vector.tensor_tensor(tanh_slot(t), tanh_slot(t), tile_in_last(t),
                                    ALU.mult).then_inc(sem["signed_ready"], 1)

        def scale_rows(q, J):
            dve.wait_ge(sem["rows_ready"], J + (NI + q * NI + 1))
            if not (q == 0 and isinstance(J, int) and J == 0):
                dve.wait_ge(sem["v_high_ready"], J + NI * (q + 1))
            f = filt[:, bass.ds(J * RC + (q // 2) * NI * RC, RC)]
            nc.vector.tensor_tensor(rows[:, :].rearrange("p (c d) -> p c d", c=RC),
                                    small[:, :].rearrange("p (c d) -> p c d", c=RC),
                                    f.rearrange("p (c o) -> p c o", o=1).to_broadcast([P, RC, D]),
                                    ALU.mult).then_inc(sem["rows_taken"], 1)

        def operand_low(q, J):
            dve.wait_ge(sem["v_high_ready"], J + (NI * (q + 1) + 1))
            if q in (0, 2):
                dve.wait_ge(sem["rows_taken"], J + (NI + q * NI + 1))
            src = small if q in (1, 3) else rows
            last = nc.vector.tensor_tensor(group(v[(q + 1) % 2][1], J), src[:, :],
                                           group(v[(q + 1) % 2][0], J), ALU.subtract)
            last.then_inc(sem["v_low_ready"], 1)
            if q == 1:
                dve.wait_ge(sem["v_low_ready"], J + (NI * (q + 1) + 1))
                dve.sem_inc(sem["rows_taken"], 1)

        def add_residual(q, J):
            if q == LAST:
                dve.wait_ge(sem["rows_ready"], J + (NI + q * NI + NI + 1))
                dve.wait_ge(sem["residual_ready"], NI + 1)
                dve.wait_ge(sem["stored"], (J + 1) * 16)
            else:
                dve.wait_ge(sem["rows_ready"], J * 2 + (NI + q * NI + 1))
                dve.wait_ge(sem["x_loaded"], (J + 1) * 16)
                dve.wait_ge(sem["residual_ready"], J + 1)
            nc.vector.tensor_tensor(rows[:, :], small[:, :], kept_part(kept, J, RESIDUAL),
                                    ALU.add).then_inc(sem["rows_taken"], 1)

        def row_stats(q, J):
            dve.wait_ge(sem["rows_taken"], J + (NI + q * NI + 1))
            for c in range(RC):
                last = nc.vector.bn_stats(stats[:, c * 6:(c + 1) * 6], rows[:, chunk(c)])
            last.then_inc(sem["stats_ready"], 1)

        def row_moments(q, J):
            n = J + (NI if q == LAST else 0)
            dve.wait_ge(sem["stats_ready"], n + 1)
            dve.sem_inc(sem["stats_seen"], 1)
            for c in range(RC):
                last = nc.vector.bn_aggr(moments[:, c * 2:(c + 1) * 2], stats[:, c * 6:(c + 1) * 6])
            last.then_inc(sem["moments_ready"], 1)
            dve.wait_ge(sem["moments_ready"], n + 1)
            nc.vector.tensor_scalar(variance[:, :].rearrange("p (c o) -> p c o", o=1),
                                    moments[:, :].rearrange("p (c o) -> p c o", o=2)[:, :, 1:2],
                                    EPS, None, ALU.add).then_inc(sem["variance_ready"], 1)

        def norm_last():
            dve.wait_ge(sem["rstd_ready"], 2 * NI)
            for c in range(RC):
                last = nc.vector.tensor_scalar(rows[:, chunk(c)], rows[:, chunk(c)],
                                               moments[:, c * 2:c * 2 + 1], rstd[:, c:c + 1],
                                               ALU.subtract, ALU.mult)
            last.then_inc(sem["last_norm_ready"], 1)

        def h4_low(J):
            dve.wait_ge(sem["h4_high_ready"], J + 1)
            nc.vector.tensor_tensor(kept_part(kept_r, J, H4_LOW), small2[:, :],
                                    kept_part(kept_r, J, H4_HIGH),
                                    ALU.subtract).then_inc(sem["h4_low_ready"], 1)

        def epilogue(q, J, t, at):
            if q in (0, 2) and t == at["take"]:
                scale_rows(q, J)
            if q in (0, 2) and t == at["split_low"]:
                operand_low(q, J)
            if q == 1 and t == at["split"]:
                operand_low(q, J)
            if q >= 3 and t == at["add"]:
                add_residual(q, J)
            if q >= 3 and t == at["stats"]:
                row_stats(q, J)
            if q >= 3 and t == at["moments"]:
                row_moments(q, J)
            if q == 3 and t == at["h4_low"]:
                h4_low(J)
            if q == 3 and t == at["hf_low"]:
                operand_low(q, J)

        for n in range(NT):
            if n in GROUP_STEPS:
                k = GROUP_STEPS.index(n)
                g = GROUP_ORDER[k]
                dve.wait_ge(sem["v_high_ready"], k + 1)
                nc.vector.tensor_tensor(group(v[0][1], g), small[:, :], group(v[0][0], g),
                                        ALU.subtract).then_inc(sem["v_low_ready"], 1)
            split_low(0, 0, n)
        dve.wait_ge(sem["v_low_ready"], NI)
        dve.sem_inc(sem["rows_taken"], NI)
        for q in range(LAST):
            if q:
                for n in range(NT):
                    split_low(q, 0, n)
                    epilogue(q - 1, NI - 1, n, AHEAD)
            with dve.Fori(0, (SHORT if q == 1 else NI) - 1) as J:
                for n in range(NT):
                    split_low(q, J + 1, n)
                    epilogue(q, J, n, AHEAD)
            if q == 1:
                with dve.Fori(SHORT - 1, NI - 1) as J:
                    for n in range(NSHORT):
                        split_low(q, J + 1, n, True)
                        epilogue(q, J, n, AHEAD)
        epilogue(3, NI - 1, -1, FIRST)
        signed(0, 0)
        for t in range(NT - 1):
            signed(0, t + 1)
            split_low(LAST, 0, t)
            epilogue(3, NI - 1, t, FIRST)
        with dve.Fori(0, NI - 1) as J:
            signed(J + 1, 0)
            split_low(LAST, J, NT - 1)
            for t in range(NT - 1):
                signed(J + 1, t + 1)
                split_low(LAST, J + 1, t)
                epilogue(LAST, J, t, CLOSE)
        split_low(LAST, NI - 1, NT - 1)
        add_residual(LAST, NI - 1)
        row_stats(LAST, NI - 1)
        row_moments(LAST, NI - 1)
        norm_last()

    @block.gpsimd
    def _(pool):
        def split_low(q, I, n):
            pool.wait_ge(sem["high_ready"], tiles_before(q, I) + (n + 1))
            nc.gpsimd.tensor_tensor(split_slot(low, n), tile_in(n, I), split_slot(high, n),
                                    ALU.subtract).then_inc(sem["pool_low_ready"], 1)

        def inverse_deviation(n):
            pool.wait_ge(sem["variance_ready"], n)
            nc.gpsimd.tensor_tensor(rstd[:, :], variance[:, :], power[:, :],
                                    ALU.pow).then_inc(sem["rstd_ready"], 1)

        def minus_mean():
            means = moments[:, :].rearrange("p (c o) -> p c o", o=2)[:, :, 0:1]
            nc.gpsimd.tensor_tensor(shift[:, :].rearrange("p (c o) -> p c o", o=1), means,
                                    minus[:, :].rearrange("p (c o) -> p c o", o=1),
                                    ALU.mult).then_inc(sem["minus_ready"], 1)

        def shift_of(n):
            inverse_deviation(n)
            minus_mean()
            pool.wait_ge(sem["rstd_ready"], n)
            pool.wait_ge(sem["minus_ready"], n)
            nc.gpsimd.tensor_tensor(shift[:, :], shift[:, :], rstd[:, :],
                                    ALU.mult).then_inc(sem["shift_ready"], 1)

        def h3_split(I, parity, count):
            pool.wait_ge(sem["h3_high_ready"], count)
            nc.gpsimd.tensor_tensor(h3_low[:, bass.ds(parity * IB, IB)], kept_part(kept, I, H3),
                                    h3_high[:, bass.ds(parity * IB, IB)],
                                    ALU.subtract).then_inc(sem["h3_low_ready"], 1)

        def residual(J):
            pool.wait_ge(sem["v_low_ready"], J + (LAST * NI + 1))
            place = kept_part(kept, J, RESIDUAL)
            nc.gpsimd.tensor_tensor(place, rows[:, :], group(v[0][0], J),
                                    ALU.add).then_inc(sem["partial_ready"], 1)
            pool.wait_ge(sem["partial_ready"], J + 1)
            nc.gpsimd.tensor_tensor(place, place, group(v[0][1], J),
                                    ALU.add).then_inc(sem["residual_ready"], 1)

        nc.gpsimd.memset(power[:, :], -0.5).then_inc(sem["power_ready"], 1)
        nc.gpsimd.memset(minus[:, :], -1.0).then_inc(sem["power_ready"], 1)
        pool.wait_ge(sem["power_ready"], 2)
        pool.sem_inc(sem["residual_ready"], 1)
        for n in POOL_STEPS:
            split_low(3, 0, n)
        with pool.Fori(0, NI - 2) as J:
            split_low(3, J + 1, POOL_STEPS[0])
            shift_of(J + 1)
            split_low(3, J + 1, POOL_STEPS[1])
            residual(J)
        split_low(3, NI - 1, POOL_STEPS[0])
        shift_of(NI - 1)
        split_low(3, NI - 1, POOL_STEPS[1])
        h3_split(0, 0, 1)
        residual(NI - 2)
        shift_of(NI)
        h3_split(1, 1, 2)
        residual(NI - 1)
        with pool.Fori(0, NI - 1) as J:
            shift_of(J + (NI + 1))
            h3_split((J + 2) % NI, J % 2, J + 3)
        inverse_deviation(2 * NI)

    block.__exit__(None, None, None)


def kernel(x, adj, L0_gnn_W1, L0_gnn_f1, L0_gnn_W2, L0_gnn_f2, L1_gnn_W1, L1_gnn_W2, L1_gnn_Wf):
    import concourse.bacc as bacc
    from concourse.bass_utils import run_bass_kernel_spmd

    x, adj = np.asarray(x), np.asarray(adj)
    tiles = adj.reshape(NI, IB, NT, TC, P).transpose(0, 2, 4, 3, 1)
    tiles = tiles[:, [0, NT - 1, *range(1, NT - 1)]].reshape(NI * NT * P, TW)
    arrays = {
        "adj": tiles,
        "x_rows": x.reshape(NI, RC, P, D).transpose(0, 2, 1, 3).reshape(NI * P, IB),
        "x_cols": x.T,
        "weights": np.concatenate([np.asarray(L0_gnn_W1), np.asarray(L0_gnn_W2), np.asarray(L1_gnn_W1).T,
                                   np.asarray(L1_gnn_W2).T, np.asarray(L1_gnn_Wf).T], axis=1),
        "filters": np.concatenate([np.asarray(f).reshape(N // P, P).T for f in (L0_gnn_f1, L0_gnn_f2)], axis=1),
        "identity": np.eye(P, dtype=np.float32),
    }
    arrays = {k: np.ascontiguousarray(a) for k, a in arrays.items()}
    nc = bacc.Bacc("TRN2", target_bir_lowering=False, num_devices=1)
    handles = {k: nc.dram_tensor(k, a.shape, F32, kind="ExternalInput").ap() for k, a in arrays.items()}
    out = nc.dram_tensor("out", (NI * P, IB), F32, kind="ExternalOutput").ap()
    build(nc, handles["adj"], handles["x_rows"], handles["x_cols"], handles["weights"],
          handles["filters"], handles["identity"], out)
    result = run_bass_kernel_spmd(nc, [arrays], core_ids=[0])
    got = result.results[0]["out"]
    return got.reshape(NI, P, RC, D).transpose(0, 2, 1, 3).reshape(N, D)
```
